# Optimizing a Trainium2 kernel written in Bass

```python
import numpy as np
import jax
import jax.numpy as jnp

def _softmax(x, axis=-1):
    return jax.nn.softmax(x, axis=axis)

def _gelu(x):
    return jax.nn.gelu(x, approximate=True)

def _silu(x):
    return jax.nn.silu(x)

def _sigmoid(x):
    return jax.nn.sigmoid(x)

def _layernorm(x, axis=-1, eps=1e-05):
    m = jnp.mean(x, axis=axis, keepdims=True)
    v = jnp.var(x, axis=axis, keepdims=True)
    return (x - m) / jnp.sqrt(v + eps)

def _scatter_add(tgt, idx, src, axis=0):
    return tgt.at[idx].add(src)

def _segment_sum(src, seg, n):
    return jax.ops.segment_sum(src, seg, n)
kernel_name = 'mk_gnn_ffn_d1_gnn_r8_b256ce'

def setup_inputs(seed: int=0):
    np.random.seed(seed)
    _w = jnp.asarray

    def _rec_inputs():
        import jax
        import jax.numpy as jnp
        _gk = jax.random.key(seed)
        x = -0.0002117 + 1 * jax.random.normal(jax.random.fold_in(_gk, 1), (6250, 256), jnp.float32)
        src = jax.random.randint(jax.random.fold_in(_gk, 2), (200000,), 0, 6250, jnp.int32)
        dst = jax.random.randint(jax.random.fold_in(_gk, 3), (200000,), 0, 6250, jnp.int32)
        _o = jnp.argsort(dst, stable=True)
        src = src[_o]
        dst = dst[_o]
        edge_weight = jax.random.uniform(jax.random.fold_in(_gk, 12), (200000,), jnp.float32, 0.0, 0.999999)
        return (x, src, dst, edge_weight)
    x, src, dst, edge_weight = _rec_inputs()

    def _L0_gnn_setup():
        import jax, jax.numpy as jnp
        import numpy as np
        IN_C, HID_C, LAT_C = (256, 64, 32)

        def gcn_conv(x, src, dst, ew, W, b):
            N = x.shape[0]
            deg = jax.ops.segment_sum(ew, dst, num_segments=N)
            dis = jnp.where(deg > 0, jax.lax.rsqrt(jnp.maximum(deg, 1e-12)), 0.0)
            norm = dis[src] * ew * dis[dst]
            h = x @ W
            out = jax.ops.segment_sum(norm[:, None] * h[src], dst, num_segments=N)
            return out + b

        def add_self_loops(edge_index, edge_weight, N, dtype):
            loop = jnp.arange(N, dtype=edge_index.dtype)
            src = jnp.concatenate([edge_index[0], loop])
            dst = jnp.concatenate([edge_index[1], loop])
            ew = jnp.concatenate([edge_weight, jnp.ones((N,), dtype=dtype)])
            return (src, dst, ew)
        key = jax.random.key(seed)
        ks = jax.random.split(key, 12)
        N, E = (12500, 156250)
        x = jax.random.normal(ks[0], (N, IN_C), dtype=jnp.float32)
        edge_index = jax.random.randint(ks[1], (2, E), 0, N, dtype=jnp.int64)
        edge_weight = jax.random.uniform(ks[2], (E,), dtype=jnp.float32)
        s = 0.05
        return {'x': x, 'edge_index': edge_index, 'edge_weight': edge_weight, 'W1': jax.random.normal(ks[3], (IN_C, HID_C), jnp.float32) * s, 'b1': jnp.zeros((HID_C,), jnp.float32), 'W2': jax.random.normal(ks[4], (HID_C, LAT_C), jnp.float32) * s, 'b2': jnp.zeros((LAT_C,), jnp.float32), 'Wd1': jax.random.normal(ks[5], (LAT_C, HID_C), jnp.float32) * s, 'bd1': jnp.zeros((HID_C,), jnp.float32), 'Wd2': jax.random.normal(ks[6], (HID_C, IN_C), jnp.float32) * s, 'bd2': jnp.zeros((IN_C,), jnp.float32)}
    _L0_gnn_all = _L0_gnn_setup()
    _L0_gnn_in = {k: v for k, v in _L0_gnn_all.items() if k in ('W1', 'b1', 'W2', 'b2', 'Wd1', 'bd1', 'Wd2', 'bd2')}
    del _L0_gnn_all

    def _L0_ffn_setup():
        import jax, jax.numpy as jnp
        import numpy as np
        B, S, D, F, E, K = (8, 256, 256, 1024, 8, 2)
        key = jax.random.key(seed)
        ks = jax.random.split(key, 10)
        s = 0.02
        return {'x': jax.random.normal(ks[0], (B, S, D), dtype=jnp.float32), 'Wr': jax.random.normal(ks[1], (D, E), dtype=jnp.float32) * s, 'W1s': jax.random.normal(ks[2], (D, F), dtype=jnp.float32) * s, 'b1s': jnp.zeros((F,), dtype=jnp.float32), 'W2s': jax.random.normal(ks[3], (F, D), dtype=jnp.float32) * s, 'b2s': jnp.zeros((D,), dtype=jnp.float32), 'W1p': jax.random.normal(ks[4], (E, D, F), dtype=jnp.float32) * s, 'b1p': jnp.zeros((E, F), dtype=jnp.float32), 'W2p': jax.random.normal(ks[5], (E, F, D), dtype=jnp.float32) * s, 'b2p': jnp.zeros((E, D), dtype=jnp.float32)}
    _L0_ffn_all = _L0_ffn_setup()
    _L0_ffn_in = {k: v for k, v in _L0_ffn_all.items() if k in ('Wr', 'W1s', 'b1s', 'W2s', 'b2s', 'W1p', 'b1p', 'W2p', 'b2p')}
    del _L0_ffn_all
    return {'x': x, 'src': src, 'dst': dst, 'edge_weight': edge_weight, 'L0_gnn_W1': _L0_gnn_in['W1'], 'L0_gnn_b1': _L0_gnn_in['b1'], 'L0_gnn_W2': _L0_gnn_in['W2'], 'L0_gnn_b2': _L0_gnn_in['b2'], 'L0_gnn_Wd1': _L0_gnn_in['Wd1'], 'L0_gnn_bd1': _L0_gnn_in['bd1'], 'L0_gnn_Wd2': _L0_gnn_in['Wd2'], 'L0_gnn_bd2': _L0_gnn_in['bd2'], 'L0_ffn_Wr': _L0_ffn_in['Wr'], 'L0_ffn_W1s': _L0_ffn_in['W1s'], 'L0_ffn_b1s': _L0_ffn_in['b1s'], 'L0_ffn_W2s': _L0_ffn_in['W2s'], 'L0_ffn_b2s': _L0_ffn_in['b2s'], 'L0_ffn_W1p': _L0_ffn_in['W1p'], 'L0_ffn_b1p': _L0_ffn_in['b1p'], 'L0_ffn_W2p': _L0_ffn_in['W2p'], 'L0_ffn_b2p': _L0_ffn_in['b2p']}

def reference(x, src, dst, edge_weight, L0_gnn_W1, L0_gnn_b1, L0_gnn_W2, L0_gnn_b2, L0_gnn_Wd1, L0_gnn_bd1, L0_gnn_Wd2, L0_gnn_bd2, L0_ffn_Wr, L0_ffn_W1s, L0_ffn_b1s, L0_ffn_W2s, L0_ffn_b2s, L0_ffn_W1p, L0_ffn_b1p, L0_ffn_W2p, L0_ffn_b2p):
    import jax
    import jax.numpy as jnp

    def _L0_gnn_ref(x, edge_index, edge_weight, W1, b1, W2, b2, Wd1, bd1, Wd2, bd2):
        import jax, jax.numpy as jnp
        import numpy as np
        IN_C, HID_C, LAT_C = (256, 64, 32)

        def gcn_conv(x, src, dst, ew, W, b):
            N = x.shape[0]
            deg = jax.ops.segment_sum(ew, dst, num_segments=N)
            dis = jnp.where(deg > 0, jax.lax.rsqrt(jnp.maximum(deg, 1e-12)), 0.0)
            norm = dis[src] * ew * dis[dst]
            h = x @ W
            out = jax.ops.segment_sum(norm[:, None] * h[src], dst, num_segments=N)
            return out + b

        def add_self_loops(edge_index, edge_weight, N, dtype):
            loop = jnp.arange(N, dtype=edge_index.dtype)
            src = jnp.concatenate([edge_index[0], loop])
            dst = jnp.concatenate([edge_index[1], loop])
            ew = jnp.concatenate([edge_weight, jnp.ones((N,), dtype=dtype)])
            return (src, dst, ew)
        N = x.shape[0]
        src, dst, ew = add_self_loops(edge_index, edge_weight, N, x.dtype)
        h = jax.nn.relu(gcn_conv(x, src, dst, ew, W1, b1))
        z = jax.nn.relu(gcn_conv(h, src, dst, ew, W2, b2))
        d = jax.nn.relu(z @ Wd1 + bd1)
        x_hat = jax.nn.sigmoid(d @ Wd2 + bd2)
        return x_hat

    def _L0_ffn_ref(x, Wr, W1s, b1s, W2s, b2s, W1p, b1p, W2p, b2p):
        import jax, jax.numpy as jnp
        import numpy as np
        B, S, D, F, E, K = (8, 256, 256, 1024, 8, 2)
        gelu = lambda t: jax.nn.gelu(t, approximate=False)
        shared = gelu(x @ W1s + b1s) @ W2s + b2s
        rw = jax.nn.softmax(x @ Wr, axis=-1)
        topw, topi = jax.lax.top_k(rw, K)
        topw = topw / jnp.sum(topw, axis=-1, keepdims=True)
        mask = jnp.sum(jax.nn.one_hot(topi, E, dtype=topw.dtype) * topw[..., None], axis=-2)
        h = gelu(jnp.einsum('bsd,edf->bsef', x, W1p) + b1p)
        priv = jnp.einsum('bsef,efd->bsed', h, W2p) + b2p
        routed = jnp.einsum('bsed,bse->bsd', priv, mask)
        return shared + routed
    edge_index = jnp.stack([src, dst])
    x = x + _L0_gnn_ref(_layernorm(x, axis=-1), edge_index, edge_weight, L0_gnn_W1, L0_gnn_b1, L0_gnn_W2, L0_gnn_b2, L0_gnn_Wd1, L0_gnn_bd1, L0_gnn_Wd2, L0_gnn_bd2)
    x = x + _L0_ffn_ref(_layernorm(x, axis=-1)[None], L0_ffn_Wr, L0_ffn_W1s, L0_ffn_b1s, L0_ffn_W2s, L0_ffn_b2s, L0_ffn_W1p, L0_ffn_b1p, L0_ffn_W2p, L0_ffn_b2p)[0]
    return x

_drawn_inputs = setup_inputs


def setup_inputs(seed=0):
    import zlib

    import numpy as np

    out = dict(_drawn_inputs(seed))
    spreads = {'L0_gnn_b1': (0.0, 0.8),
     'L0_gnn_b2': (0.0, 0.8),
     'L0_gnn_bd1': (0.0, 0.71),
     'L0_gnn_bd2': (0.0, 0.299),
     'L0_ffn_b1s': (0.0, 0.277),
     'L0_ffn_b2s': (0.0, 0.1),
     'L0_ffn_b1p': (0.0, 0.366),
     'L0_ffn_b2p': (0.0, 0.1)}
    factors = {'edge_weight': 8.0,
     'L0_gnn_W1': 8.0,
     'L0_gnn_W2': 8.0,
     'L0_gnn_Wd1': 8.0,
     'L0_gnn_Wd2': 5.221}
    for name, (base, spread) in spreads.items():
        noise = np.random.default_rng([zlib.crc32(name.encode()), seed]).standard_normal(out[name].shape)
        drawn = base * np.exp(spread * noise) if base else spread * noise
        out[name] = jnp.asarray(drawn.astype(out[name].dtype))
    for name, factor in factors.items():
        out[name] = (out[name] * factor).astype(out[name].dtype)
    return out
```

```python
import concourse.bass as bass
from concourse import mybir
from contextlib import ExitStack


def gnn_moe_kernel(nc, x, src, dst, ew, gw1, gb1, gw2, gb2, wd1, bd1, wd2, bd2,
                   wr, w1s, b1s, w2s, b2s, w1p, b1p, w2p, b2p, out):
    f32, i32, u32 = mybir.dt.float32, mybir.dt.int32, mybir.dt.uint32
    ALU, ACT, AX = mybir.AluOpType, mybir.ActivationFunctionType, mybir.AxisListType
    P = 128
    N, D = x.shape
    E = src.shape[0]
    H, L = gw2.shape
    NE = wr.shape[1]
    F = w1s.shape[1]
    KD, KF = D // P, F // P
    NB = -(-N // P)
    NP = NB * P
    LASTB = N - (NB - 1) * P
    U = 8
    ER = -(-E // P)
    NG = -(-ER // (2 * U)) * 2
    RB = -(-NG * U // P)
    FULL = E // P
    REST = E - FULL * P
    TS = 7
    NT = NB // TS
    assert NB == NT * TS and NE == 8
    EPS = 1e-5

    g1_dram = nc.dram_tensor("g1_table", (NP, H), f32).ap()
    g2_dram = nc.dram_tensor("g2_table", (NP, L), f32).ap()
    span_dram = nc.dram_tensor("span_scratch", (2, RB * P // U), i32).ap()
    vb_dram = None

    with ExitStack() as ctx:
        def sb(name, shape, dt=f32):
            return ctx.enter_context(nc.sbuf_tensor(name, shape, dt))

        def sem(name):
            return ctx.enter_context(nc.semaphore(name))

        bank = [ctx.enter_context(nc.psum_tensor(f"bank{i}", [P, 512], f32)) for i in range(8)]

        xr = sb("xr", [P, NB, D])
        xT = sb("xT", [P, KD, NP])
        srcT = sb("srcT", [P, RB * P])
        dstT = sb("dstT", [P, RB * P])
        ewT = sb("ewT", [P, RB * P])
        acc = sb("acc", [P, NB, H])
        dis = sb("dis", [P, NB])
        stat = sb("stat", [P, NB, 6])
        mv = sb("mv", [P, NB, 2])
        rstd = sb("rstd", [P, NB])
        tmp = sb("tmp", [P, NB])
        ident = sb("ident", [P, P])
        ones = sb("ones", [P, P])
        half = sb("half", [P, NB])
        spans = sb("spans", [1, 3, RB * P // U], i32)
        NGP = RB * P // U
        xn = sb("xn", [P, 2, D])

        def pow_neg_half(pool, out_, in_):
            return nc.gpsimd.tensor_tensor(out_, in_, half[:, :], ALU.pow)

        with ExitStack() as c1:
            rows = [c1.enter_context(nc.sbuf_tensor(f"rows{k}", [P, RB, P], f32)) for k in range(3)]
            irow = c1.enter_context(nc.sbuf_tensor("irow", [P, RB, P], i32))
            mm = c1.enter_context(nc.sbuf_tensor("mm", [P, 2, RB], f32))
            mmg = c1.enter_context(nc.sbuf_tensor("mmg", [RB, 2, P // U], f32))
            mmi = c1.enter_context(nc.sbuf_tensor("mmi", [RB, 2, P // U], i32))
            nvf = c1.enter_context(nc.sbuf_tensor("nvf", [1, 2, NGP], f32))
            zer = c1.enter_context(nc.sbuf_tensor("zer", [1, NGP], f32))
            s_pad, s_src, s_dst, s_ew = sem("pad_set"), sem("src_in"), sem("dst_in"), sem("ew_in")
            s_x, s_xpad, s_conv, s_id = sem("x_in"), sem("xpad_set"), sem("rows_ready"), sem("consts_set")
            s_tp, s_ev, s_mm, s_mmt = sem("edges_transposed"), sem("edges_copied"), sem("minmax_ready"), sem("minmax_transposed")
            s_blk, s_sd, s_sl, s_ch, s_ch2, s_srcc = sem("blocks_ready"), sem("span_stored"), sem("span_loaded"), sem("vchain"), sem("pchain"), sem("src_used")
            block = c1.enter_context(nc.Block())
            RBF = FULL // P
            RR = FULL - RBF * P
            xb = x[0:(NB - 1) * P, :].rearrange("(b p) d -> p b d", p=P)

            @block.sync
            def _(sp):
                def load(dst_t, src_d, s):
                    sp.dma_start(dst_t[:, 0:RBF, :], src_d[0:RBF * P * P].rearrange("(b p j) -> p b j", p=P, j=P)).then_inc(s, 16)
                    sp.dma_start(dst_t[0:RR, RBF, :], src_d[RBF * P * P:FULL * P].rearrange("(p j) -> p j", j=P)).then_inc(s, 16)
                    sp.dma_start(dst_t[RR:RR + 1, RBF, 0:REST], src_d[FULL * P:E].rearrange("(p j) -> p j", p=1)).then_inc(s, 16)
                sp.wait_ge(s_pad, 1)
                load(irow, dst, s_dst)
                sp.wait_ge(s_pad, 2)
                load(rows[2], ew, s_ew)
                sp.wait_ge(s_srcc, 1)
                load(irow, src, s_src)
                sp.wait_ge(s_xpad, 1)
                for q in range(4):
                    a, b = q * (NB - 1) // 4, (q + 1) * (NB - 1) // 4
                    sp.dma_start(xr[:, a:b, :], xb[:, a:b, :]).then_inc(s_x, 16)
                sp.dma_start(xr[0:LASTB, NB - 1, :], x[(NB - 1) * P:N, :]).then_inc(s_x, 16)
                sp.wait_ge(s_blk, 1)
                for m in range(2):
                    sp.dma_start(span_dram[m, :].rearrange("(b k) -> b k", b=RB), mmi[:, m, :]).then_inc(s_sd, 16)
                sp.wait_ge(s_sd, 32)
                sp.dma_start(spans[0:1, 0:2, :], span_dram.rearrange("(o m) g -> o m g", o=1)).then_inc(s_sl, 16)
                sp.wait_ge(s_sl, 16)

            @block.gpsimd
            def _(pool):
                pool.memset(ident[:, :], 0.0).then_inc(s_ch2, 1)
                pool.memset(ones[:, :], 1.0)
                pool.memset(half[:, :], -0.5)
                pool.memset(zer[:, :], 0.0)
                pool.wait_ge(s_ch2, 1)
                pool.affine_select(out=ident[:, :], in_=ident[:, :], compare_op=ALU.not_equal, fill=1.0,
                                   base=0, pattern=[[-1, P]], channel_multiplier=1).then_inc(s_id, 1)

            @block.vector
            def _(v):
                n = [0]

                def link(ins):
                    n[0] += 1
                    ins.then_inc(s_ch, 1)
                    v.wait_ge(s_ch, n[0])
                v.memset(irow[:, RBF, :], N - 1).then_inc(s_pad, 1)
                v.memset(rows[2][:, RBF, :], 0.0).then_inc(s_pad, 1)
                v.memset(xr[:, NB - 1, :], 0.0).then_inc(s_xpad, 1)
                v.wait_ge(s_dst, 48)
                link(v.tensor_copy(rows[1][:, :, :], irow[:, :, :]))
                v.memset(irow[:, RBF, :], 0).then_inc(s_srcc, 1)
                v.tensor_reduce(mm[:, 0, :], rows[1][:, :, :], AX.X, ALU.min)
                v.tensor_reduce(mm[:, 1, :], rows[1][:, :, :], AX.X, ALU.max).then_inc(s_mm, 1)
                v.wait_ge(s_ew, 48)
                v.wait_ge(s_src, 48)
                v.tensor_copy(rows[0][:, :, :], irow[:, :, :]).then_inc(s_conv, 1)
                v.wait_ge(s_mmt, 1)
                link(v.tensor_reduce(mmg[:, 0, :], bank[0][0:RB, 0:P].rearrange("p (g u) -> p g u", u=U), AX.X, ALU.min))
                link(v.tensor_reduce(mmg[:, 1, :], bank[0][0:RB, P:2 * P].rearrange("p (g u) -> p g u", u=U), AX.X, ALU.max))
                link(v.tensor_copy(mmi[:, :, :], mmg[:, :, :]))
                v.tensor_scalar(mmi[:, :, :], mmi[:, :, :], 7, None, ALU.arith_shift_right).then_inc(s_blk, 1)
                k = 0
                for b0 in range(0, RB, 4):
                    for a, d in enumerate((srcT, dstT, ewT)):
                        k += 1
                        v.wait_ge(s_tp, k)
                        w = min(4, RB - b0) * P
                        v.tensor_copy(d[:, b0 * P:b0 * P + w], bank[1 + (k - 1) % 4][:, 0:w]).then_inc(s_ev, 1)
                v.wait_ge(s_sl, 16)
                link(v.tensor_copy(nvf[:, :, :], spans[:, 0:2, :]))
                link(v.tensor_tensor(nvf[:, 1, :], nvf[:, 1, :], nvf[:, 0, :], ALU.subtract))
                link(v.tensor_scalar(nvf[:, 1, :], nvf[:, 1, :], 1.0, None, ALU.add))
                v.wait_ge(s_id, 1)
                link(v.tensor_tensor_scan(nvf[:, 0, :], nvf[:, 1, :], zer[:, :], 0.0, ALU.add, ALU.add))
                link(v.tensor_scalar(spans[:, 1, :], spans[:, 1, :], 1.0, None, ALU.add))
                link(v.tensor_tensor(nvf[:, 0, :], nvf[:, 0, :], nvf[:, 1, :], ALU.subtract))
                link(v.tensor_copy(nvf[:, 1, :], spans[:, 0, :]))
                link(v.tensor_tensor(nvf[:, 0, :], nvf[:, 0, :], nvf[:, 1, :], ALU.subtract))
                link(v.tensor_scalar(spans[:, 2, :], nvf[:, 0, :], float(NB), None, ALU.add))
                v.wait_ge(s_x, 80)
                for t in range(NB):
                    last = v.bn_stats(stat[:, t, :], xr[:, t, :])
                link(last)
                for t in range(NB):
                    last = v.bn_aggr(mv[:, t, :], stat[:, t, :])
                link(last)
                link(v.tensor_scalar(tmp[:, :], mv[:, :, 1], EPS, None, ALU.add))

            @block.tensor
            def _(pe):
                pe.wait_ge(s_id, 1)
                pe.wait_ge(s_mm, 1)
                pe.transpose(bank[0][0:RB, 0:P], mm[:, 0, :], ident[:, :])
                pe.transpose(bank[0][0:RB, P:2 * P], mm[:, 1, :], ident[:, :]).then_inc(s_mmt, 1)
                pe.wait_ge(s_conv, 1)
                k = 0
                for b0 in range(0, RB, 4):
                    for a in range(3):
                        k += 1
                        if k > 4:
                            pe.wait_ge(s_ev, k - 4)
                        for b in range(b0, min(b0 + 4, RB)):
                            last = pe.transpose(bank[1 + (k - 1) % 4][:, (b - b0) * P:(b - b0 + 1) * P], rows[a][:, b, :], ident[:, :])
                        last.then_inc(s_tp, 1)

        def edge_pass(name, C, table):
            with ExitStack() as c:
                oh = c.enter_context(nc.sbuf_tensor(f"oh_{name}", [P, U, P], f32))
                iota = c.enter_context(nc.sbuf_tensor(f"iota_{name}", [P, NP], f32))
                iotai = c.enter_context(nc.sbuf_tensor(f"iotai_{name}", [P, 512], i32))
                idx = c.enter_context(nc.sbuf_tensor(f"idx_{name}", [P, 2, U], u32))
                msg = c.enter_context(nc.sbuf_tensor(f"msg_{name}", [P, 2, U, C], f32))
                s_oh, s_mm, s_add = sem(f"onehots_{name}"), sem(f"sums_{name}"), sem(f"added_{name}")
                s_idx = [sem(f"idx{k}_{name}") for k in range(2)]
                s_g = [sem(f"gathered{k}_{name}") for k in range(2)]
                s_grp = sem(f"group_used_{name}")
                s_turn, s_rows = sem(f"group_started_{name}"), sem(f"rows_seen_{name}")
                s_iota, s_c = sem(f"iota_{name}"), sem(f"iotac_{name}")
                block = c.enter_context(nc.Block())

                if table is not None:
                    @block.scalar
                    def _(act):
                        with nc.scalar.Fori(0, NG // 2) as i:
                            for s in range(2):
                                act.wait_ge(s_grp, i * 2 + s + 1)
                                act.activation(idx[:, s, :], srcT[:, bass.ds((i * 2 + s) * U, U)], ACT.Copy).then_inc(s_idx[s], 1)

                @block.gpsimd
                def _(pool):
                    for k, a in enumerate(range(0, NP, 512)):
                        w = min(512, NP - a)
                        if k:
                            pool.wait_ge(s_c, k)
                        pool.iota(iotai[:, 0:w], pattern=[[1, w]], base=a, channel_multiplier=0).then_inc(s_iota, 1)
                    if table is not None:
                        with nc.gpsimd.Fori(0, NG // 2) as i:
                            for s in range(2):
                                pool.wait_ge(s_idx[s], i + 1)
                                pool.wait_ge(s_grp, i * 2 + s + 1)
                                pool.sem_inc(s_turn, 1)
                                for j in range(U):
                                    pool.indirect_dma_start(out=msg[:, s, j, :], out_offset=None, in_=table,
                                                            in_offset=bass.IndirectOffsetOnAxis(ap=idx[:, s, j:j + 1], axis=0)).then_inc(s_g[s], 16)

                def visits(eng, g):
                    first = eng.value_load(spans[0:1, 0, bass.ds(g, 1)], min_val=0, max_val=NB - 1)
                    end = eng.value_load(spans[0:1, 1, bass.ds(g, 1)], min_val=1, max_val=NB)
                    shift = eng.value_load(spans[0:1, 2, bass.ds(g, 1)], min_val=0, max_val=NG * NB + NB)
                    return first, end, shift

                @block.vector
                def _(v):
                    for k, a in enumerate(range(0, NP, 512)):
                        w = min(512, NP - a)
                        v.wait_ge(s_iota, k + 1)
                        v.tensor_copy(iota[:, a:a + w], iotai[:, 0:w]).then_inc(s_c, 1)
                    nio = -(-NP // 512)
                    v.wait_ge(s_c, nio)
                    v.sem_inc(s_grp, 2)
                    v.sem_inc(s_oh, NB)
                    v.sem_inc(s_add, NB)
                    with nc.vector.Fori(0, NG // 2) as i:
                        for s in range(2):
                            g = i * 2 + s
                            first, end, shift = visits(v, g)
                            with nc.vector.Fori(first, end) as a:
                                for j in range(U):
                                    t = g * U + j
                                    last = v.tensor_scalar(oh[:, j, :], iota[:, bass.ds(a * P, P)], dstT[:, bass.ds(t, 1)],
                                                           ewT[:, bass.ds(t, 1)], ALU.is_equal, ALU.mult)
                                last.then_inc(s_oh, 1)
                                v.wait_ge(s_mm, shift + a + 1)
                                if C == 1:
                                    d = dis[:, bass.ds(a, 1)]
                                else:
                                    d = acc[:, bass.ds(a, 1), 0:C].rearrange("p a c -> p (a c)")
                                v.tensor_tensor(d, d, bank[0][:, 0:C], ALU.add).then_inc(s_add, 1)
                                v.wait_ge(s_add, shift + a + 1)
                            v.sem_inc(s_grp, 1)

                @block.tensor
                def _(pe):
                    pe.sem_inc(s_mm, NB)
                    with nc.tensor.Fori(0, NG // 2) as i:
                        for s in range(2):
                            g = i * 2 + s
                            first, end, shift = visits(pe, g)
                            if table is not None:
                                pe.wait_ge(s_g[s], (i + 1) * (16 * U))
                                pe.sem_inc(s_rows, 1)
                            with nc.tensor.Fori(first, end) as a:
                                pe.wait_ge(s_oh, shift + a + 1)
                                for j in range(U):
                                    rhs = ones[:, 0:1] if table is None else msg[:, s, j, :]
                                    last = pe.matmul(bank[0][:, 0:C], oh[:, j, :], rhs, start=(j == 0), stop=(j == U - 1))
                                last.then_inc(s_mm, 1)

        def pow_phase(name, todo):
            with ExitStack() as c:
                s_a, s_b, s_c = sem(f"pa_{name}"), sem(f"pb_{name}"), sem(f"pc_{name}")
                block = c.enter_context(nc.Block())
                todo(block, s_a, s_b, s_c)

        def before_degrees(block, a, b, c_):
            @block.gpsimd
            def _(pool):
                pow_neg_half(pool, rstd[:, :], tmp[:, :]).then_inc(a, 1)

            @block.vector
            def _(v):
                v.memset(dis[:, :], 1.0)
        pow_phase("ln1", before_degrees)
        edge_pass("deg", 1, None)

        def degrees(block, a, b, c_):
            @block.vector
            def _(v):
                v.tensor_scalar(tmp[:, :], dis[:, :], 1e-12, None, ALU.max).then_inc(a, 1)
                v.wait_ge(a, 1)
                v.tensor_scalar(dis[:, :], dis[:, :], 0.0, None, ALU.is_gt).then_inc(c_, 1)
                v.wait_ge(b, 1)
                v.wait_ge(c_, 1)
                v.tensor_tensor(dis[:, :], dis[:, :], mv[:, :, 1], ALU.mult)

            @block.gpsimd
            def _(pool):
                pool.wait_ge(a, 1)
                pow_neg_half(pool, mv[:, :, 1], tmp[:, :]).then_inc(b, 1)
        pow_phase("deg", degrees)

        def normalise(block, name, s_extra=None):
            s_n, s_t, s_e = sem(f"normed_{name}"), sem(f"transposed_{name}"), sem(f"xT_{name}")

            @block.vector
            def _(v):
                with nc.vector.Fori(0, NT) as i:
                    for j in range(TS):
                        t = i * TS + j
                        v.wait_ge(s_t, t + 1)
                        v.tensor_scalar(xn[:, 0, :], xr[:, bass.ds(t, 1), :].rearrange("p a d -> p (a d)"),
                                        mv[:, bass.ds(t, 1), 0:1].rearrange("p a b -> p (a b)"),
                                        rstd[:, bass.ds(t, 1)], ALU.subtract, ALU.mult).then_inc(s_n, 1)

            @block.tensor
            def _(pe):
                pe.sem_inc(s_t, 1)
                with nc.tensor.Fori(0, NT) as i:
                    for j in range(TS):
                        t = i * TS + j
                        pe.wait_ge(s_n, t + 1)
                        pe.wait_ge(s_e, t + 1)
                        for k in range(KD):
                            last = pe.transpose(bank[0][:, k * P:(k + 1) * P], xn[:, 0, k * P:(k + 1) * P], ident[:, :])
                        last.then_inc(s_t, 1)

            @block.scalar
            def _(act):
                act.sem_inc(s_e, 1)
                with nc.scalar.Fori(0, NT) as i:
                    for j in range(TS):
                        t = i * TS + j
                        act.wait_ge(s_t, t + 2)
                        act.activation(xT[:, :, bass.ds(t * P, P)], bank[0][:, 0:KD * P].rearrange("p (k c) -> p k c", k=KD),
                                       ACT.Copy).then_inc(s_e, 1)

        with ExitStack() as c:
            block = c.enter_context(nc.Block())
            normalise(block, "ln1")

        def make_table(name, K, pieces, lhsT_of, w_tile, C, table):
            with ExitStack() as c:
                s_h, s_s, s_d = sem(f"rows_{name}"), sem(f"scaled_{name}"), sem(f"stored_{name}")
                block = c.enter_context(nc.Block())

                @block.tensor
                def _(pe):
                    for t in range(NB):
                        if t >= 2:
                            pe.wait_ge(s_s, t - 1)
                        for k in range(pieces):
                            last = pe.matmul(bank[t % 2][:, 0:C], lhsT_of(k, t), w_tile[0:K, k, :], start=(k == 0), stop=(k == pieces - 1))
                        last.then_inc(s_h, 1)

                @block.vector
                def _(v):
                    for t in range(NB):
                        v.wait_ge(s_h, t + 1)
                        v.tensor_scalar(acc[:, t, 0:C], bank[t % 2][:, 0:C], dis[:, t:t + 1], None, ALU.mult).then_inc(s_s, 1)

                @block.sync
                def _(sp):
                    sp.wait_ge(s_s, NB)
                    sp.dma_start(table.rearrange("(b p) c -> p b c", p=P), acc[:, :, 0:C]).then_inc(s_d, 16)
                    sp.wait_ge(s_d, 16)

        with ExitStack() as cg:
            w1t = cg.enter_context(nc.sbuf_tensor("gw1_sb", [P, KD, H], f32))
            w2t = cg.enter_context(nc.sbuf_tensor("gw2_sb", [H, 1, L], f32))
            b1row = cg.enter_context(nc.sbuf_tensor("gb1_sb", [P, H], f32))
            b2row = cg.enter_context(nc.sbuf_tensor("gb2_sb", [P, L], f32))
            wd1t = cg.enter_context(nc.sbuf_tensor("wd1_sb", [L, H], f32))
            wd2t = cg.enter_context(nc.sbuf_tensor("wd2_sb", [H + 1, D], f32))
            bd1c = cg.enter_context(nc.sbuf_tensor("bd1_sb", [H, 1], f32))
            with ExitStack() as c:
                s_w = sem("gnn_weights_in")
                block = c.enter_context(nc.Block())

                @block.sync
                def _(sp):
                    sp.dma_start(w1t[:, :, :], gw1.rearrange("(k p) h -> p k h", p=P)).then_inc(s_w, 16)
                    sp.dma_start(w2t[:, 0, :], gw2).then_inc(s_w, 16)
                    sp.dma_start(b1row[:, :], gb1.rearrange("(o h) -> o h", o=1).broadcast_to([P, H])).then_inc(s_w, 16)
                    sp.dma_start(b2row[:, :], gb2.rearrange("(o h) -> o h", o=1).broadcast_to([P, L])).then_inc(s_w, 16)
                    sp.dma_start(wd1t[:, :], wd1).then_inc(s_w, 16)
                    sp.dma_start(wd2t[0:H, :], wd2).then_inc(s_w, 16)
                    sp.dma_start(wd2t[H:H + 1, :], bd2.rearrange("(o h) -> o h", o=1)).then_inc(s_w, 16)
                    sp.dma_start(bd1c[:, :], bd1.rearrange("(h o) -> h o", o=1)).then_inc(s_w, 16)
                    sp.wait_ge(s_w, 128)

            make_table("g1", P, KD, lambda k, t: xT[:, k, t * P:(t + 1) * P], w1t, H, g1_dram)
            edge_pass("c1", H, g1_dram)

            hT = xT[:, 0, :]

            def finish_conv(name, C, brow):
                with ExitStack() as c:
                    s_c, s_t, s_e = sem(f"relu_{name}"), sem(f"hT_psum_{name}"), sem(f"hT_{name}")
                    block = c.enter_context(nc.Block())

                    @block.vector
                    def _(v):
                        a = acc[:, :, 0:C]
                        v.tensor_tensor(a, a, dis[:, :].unsqueeze(2).broadcast_to([P, NB, C]), ALU.mult).then_inc(s_c, 1)
                        v.wait_ge(s_c, 1)
                        v.tensor_tensor(a, a, brow[:, :].unsqueeze(1).broadcast_to([P, NB, C]), ALU.add).then_inc(s_c, 1)
                        v.wait_ge(s_c, 2)
                        v.tensor_scalar(a, a, 0.0, None, ALU.max).then_inc(s_c, 1)

                    @block.tensor
                    def _(pe):
                        pe.wait_ge(s_c, 3)
                        for q, t0 in enumerate(range(0, NB, 4)):
                            if q >= 2:
                                pe.wait_ge(s_e, q - 1)
                            for t in range(t0, min(t0 + 4, NB)):
                                last = pe.transpose(bank[q % 2][0:C, (t - t0) * P:(t - t0 + 1) * P], acc[:, t, 0:C], ident[:, :])
                            last.then_inc(s_t, 1)

                    @block.scalar
                    def _(act):
                        for q, t0 in enumerate(range(0, NB, 4)):
                            w = min(4, NB - t0) * P
                            act.wait_ge(s_t, q + 1)
                            act.activation(hT[0:C, t0 * P:t0 * P + w], bank[q % 2][0:C, 0:w], ACT.Copy).then_inc(s_e, 1)

            finish_conv("c1", H, b1row)
            make_table("g2", H, 1, lambda k, t: hT[0:H, t * P:(t + 1) * P], w2t, L, g2_dram)
            edge_pass("c2", L, g2_dram)
            finish_conv("c2", L, b2row)

            with ExitStack() as c:
                s_d, s_dr, s_y, s_sg, s_x1, s_st = sem("d_psum"), sem("d_relu"), sem("xhat_psum"), sem("sigmoid"), sem("x1"), sem("stats2")
                s_one, s_pw = sem("ones_row"), sem("rstd2")
                sg = c.enter_context(nc.sbuf_tensor("sg", [P, 2, D], f32))
                block = c.enter_context(nc.Block())
                dT = xT[:, 1, :]
                NQ = -(-NP // 512)

                @block.tensor
                def _(pe):
                    for q in range(NQ):
                        w = min(512, NP - q * 512)
                        if q >= 2:
                            pe.wait_ge(s_dr, q - 1)
                        pe.matmul(bank[q % 2][0:H, 0:w], wd1t[:, :], hT[0:L, q * 512:q * 512 + w], start=True, stop=True).then_inc(s_d, 1)
                    pe.wait_ge(s_one, 1)
                    pe.wait_ge(s_dr, NQ)
                    for t in range(NB):
                        if t >= 2:
                            pe.wait_ge(s_sg, t - 1)
                        pe.matmul(bank[2 + t % 2][:, 0:D], dT[0:H + 1, t * P:(t + 1) * P], wd2t[:, :], start=True, stop=True).then_inc(s_y, 1)

                @block.scalar
                def _(act):
                    for q in range(NQ):
                        w = min(512, NP - q * 512)
                        act.wait_ge(s_d, q + 1)
                        act.activation(dT[0:H, q * 512:q * 512 + w], bank[q % 2][0:H, 0:w], ACT.Relu, bias=bd1c[:, :]).then_inc(s_dr, 1)
                    for t in range(NB):
                        act.wait_ge(s_y, t + 1)
                        if t >= 2:
                            act.wait_ge(s_x1, t - 1)
                        act.activation(sg[:, t % 2, :], bank[2 + t % 2][:, 0:D], ACT.Sigmoid).then_inc(s_sg, 1)

                @block.vector
                def _(v):
                    v.memset(dT[H:H + 1, :], 1.0).then_inc(s_one, 1)
                    for t in range(NB):
                        v.wait_ge(s_sg, t + 1)
                        v.tensor_tensor(xr[:, t, :], xr[:, t, :], sg[:, t % 2, :], ALU.add).then_inc(s_x1, 1)
                    v.wait_ge(s_x1, NB)
                    for t in range(NB):
                        last = v.bn_stats(stat[:, t, :], xr[:, t, :])
                    last.then_inc(s_st, 1)
                    v.wait_ge(s_st, 1)
                    for t in range(NB):
                        last = v.bn_aggr(mv[:, t, :], stat[:, t, :])
                    last.then_inc(s_st, 1)
                    v.wait_ge(s_st, 2)
                    v.tensor_scalar(tmp[:, :], mv[:, :, 1], EPS, None, ALU.add).then_inc(s_st, 1)

                @block.gpsimd
                def _(pool):
                    pool.wait_ge(s_st, 3)
                    pow_neg_half(pool, rstd[:, :], tmp[:, :]).then_inc(s_pw, 1)

        with ExitStack() as c:
            block = c.enter_context(nc.Block())
            normalise(block, "ln2")

        mask = sb("mask", [P, NB, NE + 1])
        b1t = sb("b1t", [P, (NE + 1) * KF])
        with ExitStack() as c:
            wrt = c.enter_context(nc.sbuf_tensor("wr_sb", [P, KD, NE], f32))
            lg = c.enter_context(nc.sbuf_tensor("lg", [P, NB, NE], f32))
            m8 = c.enter_context(nc.sbuf_tensor("m8", [P, NB, NE], f32))
            i8 = c.enter_context(nc.sbuf_tensor("i8", [P, NB, NE], u32))
            i8f = c.enter_context(nc.sbuf_tensor("i8f", [P, NB, 2], f32))
            dl = c.enter_context(nc.sbuf_tensor("dl", [P, NB, 2], f32))
            wt = c.enter_context(nc.sbuf_tensor("wt", [P, NB, 2], f32))
            eq = c.enter_context(nc.sbuf_tensor("eq", [P, 2, NB, NE], f32))
            ei = c.enter_context(nc.sbuf_tensor("ei", [P, NE], i32))
            ef = c.enter_context(nc.sbuf_tensor("ef", [P, NE], f32))
            b1r = c.enter_context(nc.sbuf_tensor("b1r", [(NE + 1) * KF, P], f32))
            s_bt = sem("biases_transposed")
            s_w, s_l, s_i, s_ch, s_dl, s_wt = sem("wr_in"), sem("logits"), sem("expert_ids"), sem("routerchain"), sem("gap"), sem("topw")
            block = c.enter_context(nc.Block())

            @block.sync
            def _(sp):
                sp.dma_start(wrt[:, :, :], wr.rearrange("(k p) e -> p k e", p=P)).then_inc(s_w, 16)
                sp.dma_start(b1r[0:NE * KF, :], b1p.rearrange("e (k p) -> (e k) p", p=P)).then_inc(s_w, 16)
                sp.dma_start(b1r[NE * KF:(NE + 1) * KF, :], b1s.rearrange("(k p) -> k p", p=P)).then_inc(s_w, 16)

            @block.gpsimd
            def _(pool):
                pool.iota(ei[:, :], pattern=[[1, NE]], base=0, channel_multiplier=0).then_inc(s_i, 1)

            @block.tensor
            def _(pe):
                pe.wait_ge(s_w, 48)
                pe.transpose(bank[1][:, 0:(NE + 1) * KF], b1r[:, :], ident[0:(NE + 1) * KF, 0:(NE + 1) * KF]).then_inc(s_bt, 1)
                for t in range(NB):
                    for k in range(KD):
                        last = pe.matmul(bank[0][:, t * NE:(t + 1) * NE], xT[:, k, t * P:(t + 1) * P], wrt[:, k, :], start=(k == 0), stop=(k == KD - 1))
                last.then_inc(s_l, 1)

            @block.scalar
            def _(act):
                act.wait_ge(s_dl, 1)
                act.activation(wt[:, :, :], dl[:, :, :], ACT.Sigmoid).then_inc(s_wt, 1)

            @block.vector
            def _(v):
                n = [0]

                def link(ins):
                    n[0] += 1
                    ins.then_inc(s_ch, 1)
                    v.wait_ge(s_ch, n[0])
                v.wait_ge(s_bt, 1)
                v.tensor_copy(b1t[:, :], bank[1][:, 0:(NE + 1) * KF])
                v.wait_ge(s_l, 1)
                link(v.tensor_copy(lg[:, :, :], bank[0][:, 0:NB * NE].rearrange("p (t e) -> p t e", e=NE)))
                for t in range(NB):
                    last = v.max(m8[:, t, :], lg[:, t, :])
                link(last)
                for t in range(NB):
                    last = v.max_index(i8[:, t, :], m8[:, t, :], lg[:, t, :])
                link(last)
                link(v.tensor_copy(i8f[:, :, :], i8[:, :, 0:2]))
                link(v.tensor_tensor(dl[:, :, 0], m8[:, :, 0], m8[:, :, 1], ALU.subtract))
                v.tensor_tensor(dl[:, :, 1], m8[:, :, 1], m8[:, :, 0], ALU.subtract).then_inc(s_dl, 1)
                v.wait_ge(s_i, 1)
                link(v.tensor_copy(ef[:, :], ei[:, :]))
                v.wait_ge(s_wt, 1)
                for k in range(2):
                    q = eq[:, k, :, :]
                    link(v.tensor_tensor(q, ef[:, :].unsqueeze(1).broadcast_to([P, NB, NE]), i8f[:, :, k:k + 1].broadcast_to([P, NB, NE]), ALU.is_equal))
                    link(v.tensor_tensor(q, q, wt[:, :, k:k + 1].broadcast_to([P, NB, NE]), ALU.mult))
                link(v.tensor_tensor(mask[:, :, 0:NE], eq[:, 0, :, :], eq[:, 1, :, :], ALU.add))
                v.memset(mask[:, :, NE:NE + 1], 1.0)

        with ExitStack() as c:
            w1t = c.enter_context(nc.sbuf_tensor("w1_sb", [P, 2, KD, F], f32))
            w2t = c.enter_context(nc.sbuf_tensor("w2_sb", [P, 2, KF, D], f32))
            b2t = c.enter_context(nc.sbuf_tensor("b2_sb", [1, NE + 1, D], f32))
            hh = c.enter_context(nc.sbuf_tensor("hh", [P, 2, KF, P], f32))
            s_w = [sem(f"expert_in{k}") for k in range(2)]
            s_b = sem("biases_in")
            s_h, s_gl, s_y, s_yd, s_o = sem("h_psum"), sem("gelu"), sem("y_psum"), sem("y_added"), sem("out_stored")
            block = c.enter_context(nc.Block())
            NX = NE + 1

            @block.sync
            def _(sp):
                sp.dma_start(b2t[:, 0:NE, :], b2p.rearrange("(o e) d -> o e d", o=1)).then_inc(s_b, 16)
                sp.dma_start(b2t[:, NE, :], b2s.rearrange("(o d) -> o d", o=1)).then_inc(s_b, 16)
                for e in range(NX):
                    if e >= 2:
                        sp.wait_ge(s_y, NB * (e - 1))
                    a, b = (w1p[e], w2p[e]) if e < NE else (w1s, w2s)
                    sp.dma_start(w1t[:, e % 2, :, :], a.rearrange("(k p) f -> p k f", p=P)).then_inc(s_w[e % 2], 16)
                    sp.dma_start(w2t[:, e % 2, :, :], b.rearrange("(k p) d -> p k d", p=P)).then_inc(s_w[e % 2], 16)
                sp.wait_ge(s_yd, NB * NX + 2)
                sp.dma_start(out[0:(NB - 1) * P, :].rearrange("(b p) d -> p b d", p=P), xr[:, 0:NB - 1, :]).then_inc(s_o, 16)
                sp.dma_start(out[(NB - 1) * P:N, :], xr[0:LASTB, NB - 1, :]).then_inc(s_o, 16)
                sp.wait_ge(s_o, 32)

            @block.tensor
            def _(pe):
                pe.wait_ge(s_b, 32)

                def up(e, n, t):
                    s = e % 2
                    r = slot(n)
                    pe.wait_ge(s_gl, n + 1)
                    for f in range(KF):
                        for k in range(KD):
                            last = pe.matmul(bank[2 * r + f // 4][:, (f % 4) * P:(f % 4 + 1) * P], w1t[:, s, k, f * P:(f + 1) * P],
                                             xT[:, k, bass.ds(t * P, P)], start=(k == 0), stop=(k == KD - 1))
                    last.then_inc(s_h, 1)

                def down(e, n):
                    s = e % 2
                    r = slot(n)
                    pe.wait_ge(s_gl, n + 3)
                    pe.wait_ge(s_yd, n + 1)
                    for f in range(KF):
                        pe.matmul(bank[4 + r][:, 0:D], hh[:, r, f, :], w2t[:, s, f, :], start=(f == 0), stop=False)
                    pe.matmul(bank[4 + r][:, 0:D], ones[0:1, :], b2t[0:1, e, :], start=False, stop=True).then_inc(s_y, 1)

                for e in range(NX):
                    pe.wait_ge(s_w[e % 2], 32 * (e // 2 + 1))
                    base = e * NB
                    cur = [base % 2]
                    slot = lambda n: cur[0]
                    up(e, base, 0)
                    with nc.tensor.Fori(0, (NB - 1) // 2) as i:
                        for j in range(2):
                            cur[0] = (base + j + 1) % 2
                            up(e, i * 2 + (base + j + 1), i * 2 + j + 1)
                            cur[0] = (base + j) % 2
                            down(e, i * 2 + (base + j))
                    cur[0] = (base + NB - 1) % 2
                    down(e, base + NB - 1)

            def tiles(eng, body):
                for e in range(NX):
                    base = e * NB
                    with eng.Fori(0, (NB - 1) // 2) as i:
                        for j in range(2):
                            body(e, (base + j) % 2, i * 2 + (base + j), i * 2 + j)
                    body(e, (base + NB - 1) % 2, base + NB - 1, NB - 1)

            @block.scalar
            def _(act):
                act.sem_inc(s_gl, 2)

                def body(e, r, n, t):
                    act.wait_ge(s_h, n + 1)
                    if not isinstance(n, int) or n >= 2:
                        act.wait_ge(s_yd, n + 1)
                    for f in range(KF):
                        last = act.activation(hh[:, r, f, :], bank[2 * r + f // 4][:, (f % 4) * P:(f % 4 + 1) * P], ACT.Gelu,
                                              bias=b1t[:, e * KF + f:e * KF + f + 1])
                    last.then_inc(s_gl, 1)
                tiles(nc.scalar, body)

            @block.vector
            def _(v):
                v.sem_inc(s_yd, 2)

                def body(e, r, n, t):
                    v.wait_ge(s_y, n + 1)
                    o = xr[:, bass.ds(t, 1), :].rearrange("p a d -> p (a d)")
                    v.scalar_tensor_tensor(out=o, in0=bank[4 + r][:, 0:D], scalar=mask[:, bass.ds(t, 1), e:e + 1].rearrange("p a b -> p (a b)"),
                                           in1=o, op0=ALU.mult, op1=ALU.add).then_inc(s_yd, 1)
                tiles(nc.vector, body)


_INS = ['x', 'src', 'dst', 'edge_weight', 'L0_gnn_W1', 'L0_gnn_b1', 'L0_gnn_W2', 'L0_gnn_b2', 'L0_gnn_Wd1', 'L0_gnn_bd1',
        'L0_gnn_Wd2', 'L0_gnn_bd2', 'L0_ffn_Wr', 'L0_ffn_W1s', 'L0_ffn_b1s', 'L0_ffn_W2s', 'L0_ffn_b2s', 'L0_ffn_W1p',
        'L0_ffn_b1p', 'L0_ffn_W2p', 'L0_ffn_b2p']


def kernel(**inputs):
    import numpy as _np
    import concourse.bacc as _bacc
    from concourse import mybir as _mybir
    from concourse.bass_utils import run_bass_kernel_spmd as _run

    nc = _bacc.Bacc("TRN2", target_bir_lowering=False, num_devices=1)
    arrays, args = {}, []
    for name in _INS:
        a = _np.ascontiguousarray(inputs[name])
        arrays[f"in_{name}_dram"] = a
        args.append(nc.dram_tensor(f"in_{name}_dram", a.shape, _mybir.dt.from_np(a.dtype), kind="ExternalInput").ap())
    shape = inputs['x'].shape
    args.append(nc.dram_tensor("out_0_dram", tuple(shape), _mybir.dt.float32, kind="ExternalOutput").ap())
    gnn_moe_kernel(nc, *args)
    r = _run(nc, [arrays], core_ids=[0])
    return r.results[0]["out_0_dram"]
```

```python
import concourse.bass as bass
from concourse import mybir
from contextlib import ExitStack


def gnn_moe_kernel(nc, x, src, dst, ew, gw1, gb1, gw2, gb2, wd1, bd1, wd2, bd2,
                   wr, w1s, b1s, w2s, b2s, w1p, b1p, w2p, b2p, out):
    f32, i32, u32, bf16 = mybir.dt.float32, mybir.dt.int32, mybir.dt.uint32, mybir.dt.bfloat16
    ALU, ACT, AX = mybir.AluOpType, mybir.ActivationFunctionType, mybir.AxisListType
    P = 128
    N, D = x.shape
    E = src.shape[0]
    H, L = gw2.shape
    NE = wr.shape[1]
    F = w1s.shape[1]
    KD, KF = D // P, F // P
    NB = -(-N // P)
    NP = NB * P
    LASTB = N - (NB - 1) * P
    UC, UD, UQ = 8, 28, 4
    NTILE = -(-E // (P * 2 * 56)) * 112
    RB = -(-NTILE // P)
    NQ4 = NTILE // UQ
    assert NTILE % (2 * UC) == 0 and NTILE % (2 * UD) == 0
    FULL = E // P
    REST = E - FULL * P
    TS = 7
    NT = NB // TS
    assert NB == NT * TS and NE == 8
    EPS = 1e-5

    g1_dram = nc.dram_tensor("g1_table", (NP, H), f32).ap()
    g2_dram = nc.dram_tensor("g2_table", (NP, L), f32).ap()
    span_dram = nc.dram_tensor("span_scratch", (2, RB * P // UQ), i32).ap()
    UT = 2 * P
    UMAX = N * 2 // UT + NE
    x_dram = nc.dram_tensor("expert_rows", ((UMAX + 1) * UT, D), f32).ap()
    y_dram = nc.dram_tensor("expert_results", ((UMAX + 1) * UT, D), f32).ap()

    with ExitStack() as ctx:
        graph = ExitStack()

        def sb(name, shape, dt=f32):
            return ctx.enter_context(nc.sbuf_tensor(name, shape, dt))

        def sbg(name, shape, dt=f32):
            return graph.enter_context(nc.sbuf_tensor(name, shape, dt))

        def sem(name):
            return ctx.enter_context(nc.semaphore(name))

        sums = ctx.enter_context(nc.psum_tensor("psum", [P, 8 * 512], f32))
        bank = [sums[:, i * 512:(i + 1) * 512] for i in range(8)]

        xr = sb("xr", [P, NB, D])
        xT = sb("xT", [P, KD, NP])
        tri = sb("tri", [P, P])
        ones = sb("ones", [P, P])
        ident = sb("ident", [P, P])
        valid = sb("valid", [P, 1])
        mv = sb("mv", [P, NB, 2])
        rstd = sb("rstd", [P, NB])
        b1t = sb("b1t", [P, (NE + 1) * KF])
        topw = sb("topw", [P, NB, 2])
        slots = sb("slots", [P, NB, 2])
        ends = sb("ends", [1, NE], i32)
        edges = sbg("edges", [P, 3, RB * P])
        iota = sbg("iota", [P, P])
        base = sbg("base", [P, NB])
        acc = sbg("acc", [P, NB * H])

        def acc_of(C):
            return acc[:, 0:NB * C].rearrange("p (b c) -> p b c", c=C)
        dis = sbg("dis", [P, NB])
        stat = sbg("stat", [P, NB, 6])
        tmp = sbg("tmp", [P, NB])
        half = sbg("half", [P, NB])
        spans = [sbg("spans_layer", [1, 3, NTILE // UC], i32), sbg("spans_degrees", [1, 3, NTILE // UD], i32)]
        wparts = sbg("wparts", [P, NTILE, 4], bf16)
        self_h = sbg("self_h", [P, NB, 4], bf16)
        iotah = sbg("iotah", [P, P], bf16)
        identh = sbg("identh", [P, P], bf16)
        xn = sbg("xn", [P, 2, D])

        def pow_neg_half(pool, out_, in_):
            return nc.gpsimd.tensor_tensor(out_, in_, half[:, :], ALU.pow)

        with ExitStack() as c1:
            rows = [c1.enter_context(nc.sbuf_tensor(f"rows{k}", [P, RB, P], f32)) for k in range(3)]
            irow = c1.enter_context(nc.sbuf_tensor("irow", [P, RB, P], i32))
            mm = c1.enter_context(nc.sbuf_tensor("mm", [P, 2, RB], f32))
            mmg = c1.enter_context(nc.sbuf_tensor("mmg", [RB, 2, P // UQ], f32))
            mmi = c1.enter_context(nc.sbuf_tensor("mmi", [RB, 2, P // UQ], i32))
            q4 = c1.enter_context(nc.sbuf_tensor("q4", [1, 2, RB * P // UQ], i32))
            q4f = c1.enter_context(nc.sbuf_tensor("q4f", [1, 2, NQ4], f32))
            nvf = c1.enter_context(nc.sbuf_tensor("nvf", [1, 4, NTILE // UC], f32))
            rest = c1.enter_context(nc.sbuf_tensor("rest", [P, NTILE], f32))
            iotai = c1.enter_context(nc.sbuf_tensor("iotai", [P, P + NB], i32))
            zer = c1.enter_context(nc.sbuf_tensor("zer", [1, NTILE // UC], f32))
            s_pad, s_src, s_dst, s_ew = sem("pad_set"), sem("src_in"), sem("dst_in"), sem("ew_in")
            s_x, s_xpad, s_conv, s_id = sem("x_in"), sem("xpad_set"), sem("rows_ready"), sem("consts_set")
            s_tp, s_ev, s_mm, s_mmt = sem("edges_transposed"), sem("edges_copied"), sem("minmax_ready"), sem("minmax_transposed")
            s_blk, s_sd, s_sl, s_ch, s_ch2, s_srcc = sem("blocks_ready"), sem("span_stored"), sem("span_loaded"), sem("vchain"), sem("pchain"), sem("src_used")
            block = c1.enter_context(nc.Block())
            RBF = FULL // P
            RR = FULL - RBF * P
            xb = x[0:(NB - 1) * P, :].rearrange("(b p) d -> p b d", p=P)

            @block.sync
            def _(sp):
                def load(dst_t, src_d, s):
                    sp.dma_start(dst_t[:, 0:RBF, :], src_d[0:RBF * P * P].rearrange("(b p j) -> p b j", p=P, j=P)).then_inc(s, 16)
                    sp.dma_start(dst_t[0:RR, RBF, :], src_d[RBF * P * P:FULL * P].rearrange("(p j) -> p j", j=P)).then_inc(s, 16)
                    sp.dma_start(dst_t[RR:RR + 1, RBF, 0:REST], src_d[FULL * P:E].rearrange("(p j) -> p j", p=1)).then_inc(s, 16)
                sp.wait_ge(s_pad, 1)
                load(irow, dst, s_dst)
                sp.wait_ge(s_pad, 2)
                load(rows[2], ew, s_ew)
                sp.wait_ge(s_srcc, 1)
                load(irow, src, s_src)
                sp.wait_ge(s_xpad, 1)
                for q in range(4):
                    a, b = q * (NB - 1) // 4, (q + 1) * (NB - 1) // 4
                    sp.dma_start(xr[:, a:b, :], xb[:, a:b, :]).then_inc(s_x, 16)
                sp.dma_start(xr[0:LASTB, NB - 1, :], x[(NB - 1) * P:N, :]).then_inc(s_x, 16)
                sp.wait_ge(s_blk, 1)
                for m in range(2):
                    sp.dma_start(span_dram[m, :].rearrange("(b k) -> b k", b=RB), mmi[:, m, :]).then_inc(s_sd, 16)
                sp.wait_ge(s_sd, 32)
                sp.dma_start(q4[:, :, :], span_dram.rearrange("(o m) g -> o m g", o=1)).then_inc(s_sl, 16)
                sp.wait_ge(s_sl, 16)

            @block.gpsimd
            def _(pool):
                pool.memset(ident[:, :], 0.0)
                pool.memset(ones[:, :], 1.0)
                pool.memset(half[:, :], -0.5)
                pool.memset(zer[:, :], 0.0)
                pool.memset(tri[:, :], 1.0)
                pool.memset(valid[:, :], 1.0)
                pool.iota(iotai[:, 0:P], pattern=[[1, P]], base=0, channel_multiplier=0)
                pool.iota(iotai[:, P:P + NB], pattern=[[P, NB]], base=0, channel_multiplier=0).then_inc(s_ch2, 1)
                pool.wait_ge(s_ch2, 1)
                pool.affine_select(out=tri[:, :], in_=tri[:, :], compare_op=ALU.is_gt, fill=0.0,
                                   base=0, pattern=[[1, P]], channel_multiplier=-1)
                pool.affine_select(out=valid[:, :], in_=valid[:, :], compare_op=ALU.is_ge, fill=0.0,
                                   base=LASTB - 1, pattern=[[0, 1]], channel_multiplier=-1)
                pool.affine_select(out=ident[:, :], in_=ident[:, :], compare_op=ALU.not_equal, fill=1.0,
                                   base=0, pattern=[[-1, P]], channel_multiplier=1).then_inc(s_id, 1)

            @block.vector
            def _(v):
                n = [0]

                def link(ins):
                    n[0] += 1
                    ins.then_inc(s_ch, 1)
                    v.wait_ge(s_ch, n[0])
                v.memset(irow[:, RBF, :], N - 1).then_inc(s_pad, 1)
                v.memset(rows[2][:, RBF, :], 0.0).then_inc(s_pad, 1)
                v.memset(xr[:, NB - 1, :], 0.0).then_inc(s_xpad, 1)
                v.wait_ge(s_dst, 48)
                link(v.tensor_copy(rows[1][:, :, :], irow[:, :, :]))
                v.memset(irow[:, RBF, :], 0).then_inc(s_srcc, 1)
                v.tensor_reduce(mm[:, 0, :], rows[1][:, :, :], AX.X, ALU.min)
                v.tensor_reduce(mm[:, 1, :], rows[1][:, :, :], AX.X, ALU.max).then_inc(s_mm, 1)
                v.wait_ge(s_ew, 48)
                v.wait_ge(s_src, 48)
                v.tensor_copy(rows[0][:, :, :], irow[:, :, :]).then_inc(s_conv, 1)
                v.wait_ge(s_mmt, 1)
                link(v.tensor_reduce(mmg[:, 0, :], bank[0][0:RB, 0:P].rearrange("p (g u) -> p g u", u=UQ), AX.X, ALU.min))
                link(v.tensor_reduce(mmg[:, 1, :], bank[0][0:RB, P:2 * P].rearrange("p (g u) -> p g u", u=UQ), AX.X, ALU.max))
                link(v.tensor_copy(mmi[:, :, :], mmg[:, :, :]))
                v.tensor_scalar(mmi[:, :, :], mmi[:, :, :], 7, None, ALU.arith_shift_right).then_inc(s_blk, 1)
                k = 0
                for b0 in range(0, RB, 4):
                    for a in range(3):
                        k += 1
                        v.wait_ge(s_tp, k)
                        w = min(4, RB - b0) * P
                        v.tensor_copy(edges[:, a, b0 * P:b0 * P + w], bank[1 + (k - 1) % 4][:, 0:w]).then_inc(s_ev, 1)
                v.wait_ge(s_sl, 16)
                link(v.tensor_copy(q4f[:, :, :], q4[:, :, 0:NQ4]))
                v.wait_ge(s_id, 1)
                for tab, u in zip(spans, (UC, UD)):
                    G = NTILE // u
                    first, last, before, more = (nvf[:, k, 0:G] for k in range(4))
                    link(v.tensor_reduce(first, q4f[:, 0, :].rearrange("p (g u) -> p g u", u=u // UQ), AX.X, ALU.min))
                    link(v.tensor_reduce(last, q4f[:, 1, :].rearrange("p (g u) -> p g u", u=u // UQ), AX.X, ALU.max))
                    link(v.tensor_copy(tab[:, 0, :], first))
                    link(v.tensor_scalar(tab[:, 1, :], last, 1.0, None, ALU.add))
                    link(v.tensor_tensor(more, last, first, ALU.subtract))
                    link(v.tensor_tensor_scan(before, more, zer[:, 0:G], 0.0, ALU.add, ALU.add))
                    link(v.tensor_tensor(before, before, more, ALU.subtract))
                    link(v.tensor_tensor(before, before, first, ALU.subtract))
                    link(v.tensor_scalar(tab[:, 2, :], before, float(NB), None, ALU.add))
                w = edges[:, 2, 0:NTILE]
                v.memset(wparts[:, :, 3], 0.0)
                link(v.tensor_copy(wparts[:, :, 0], w))
                link(v.tensor_tensor(rest[:, :], w, wparts[:, :, 0], ALU.subtract))
                link(v.tensor_copy(wparts[:, :, 1], rest[:, :]))
                v.tensor_tensor(wparts[:, :, 2], rest[:, :], wparts[:, :, 1], ALU.subtract)
                link(v.memset(self_h[:, :, :], 0.0))
                v.memset(self_h[:, :, 0], 1.0)
                v.tensor_copy(iotah[:, :], iotai[:, 0:P])
                v.tensor_copy(identh[:, :], ident[:, :])
                v.wait_ge(s_x, 80)
                for t in range(NB):
                    last = v.bn_stats(stat[:, t, :], xr[:, t, :])
                link(last)
                for t in range(NB):
                    last = v.bn_aggr(mv[:, t, :], stat[:, t, :])
                link(last)
                link(v.tensor_scalar(tmp[:, :], mv[:, :, 1], EPS, None, ALU.add))
                v.tensor_copy(iota[:, :], iotai[:, 0:P])
                v.tensor_copy(base[:, :], iotai[:, P:P + NB])

            @block.tensor
            def _(pe):
                pe.wait_ge(s_id, 1)
                pe.wait_ge(s_mm, 1)
                pe.transpose(bank[0][0:RB, 0:P], mm[:, 0, :], ident[:, :])
                pe.transpose(bank[0][0:RB, P:2 * P], mm[:, 1, :], ident[:, :]).then_inc(s_mmt, 1)
                pe.wait_ge(s_conv, 1)
                k = 0
                for b0 in range(0, RB, 4):
                    for a in range(3):
                        k += 1
                        if k > 4:
                            pe.wait_ge(s_ev, k - 4)
                        for b in range(b0, min(b0 + 4, RB)):
                            last = pe.transpose(bank[1 + (k - 1) % 4][:, (b - b0) * P:(b - b0 + 1) * P], rows[a][:, b, :], ident[:, :])
                        last.then_inc(s_tp, 1)

        def edge_pass(name, C, stride, U, table, dt):
            groups = NTILE // U
            deg = table is None
            self_rows = self_h[:, :, :].rearrange("p b c -> p (b c)") if deg else acc[:, 0:NB * C]
            which = 0 if U == UC else 1
            with ExitStack() as c:
                oh = [c.enter_context(nc.sbuf_tensor(f"oh{k}_{name}", [P, U, P], dt)) for k in range(3)]
                rel = c.enter_context(nc.sbuf_tensor(f"rel_{name}", [P, 3, U], f32))
                cols = c.enter_context(nc.sbuf_tensor(f"cols_{name}", [P, 2, 2, U], f32))
                if deg:
                    msg = c.enter_context(nc.sbuf_tensor(f"msg_{name}", [P, 2, U, 4], dt))
                else:
                    idx = c.enter_context(nc.sbuf_tensor(f"idx_{name}", [P, 2, U], u32))
                    msg = c.enter_context(nc.sbuf_tensor(f"msg_{name}", [P, 2, U, C], f32))
                s_rel, s_oh, s_mm = ([sem(f"{w}{k}_{name}") for k in range(3)] for w in ("relative", "onehots", "summed"))
                s_idx, s_cols, s_init = sem(f"idx_{name}"), sem(f"cols_{name}"), sem(f"sums_started_{name}")
                s_g = [sem(f"gathered{k}_{name}") for k in range(2)]
                s_vec, s_pe = sem(f"cols_used_{name}"), sem(f"rows_used_{name}")
                s_turn, s_rows, s_seen = sem(f"group_started_{name}"), sem(f"rows_seen_{name}"), sem(f"cols_seen_{name}")
                block = c.enter_context(nc.Block())

                @block.scalar
                def _(act):
                    with nc.scalar.Fori(0, groups // 2) as i:
                        for s in range(2):
                            g = i * 2 + s
                            act.wait_ge(s_vec, g + 1)
                            act.activation(cols[:, s, :, :], edges[:, 1:3, bass.ds(g * U, U)], ACT.Copy).then_inc(s_cols, 1)
                            act.wait_ge(s_pe, g + 1)
                            if deg:
                                act.activation(msg[:, s, :, :], wparts[:, bass.ds(g * U, U), :], ACT.Copy).then_inc(s_idx, 1)
                            else:
                                act.activation(idx[:, s, :], edges[:, 0, bass.ds(g * U, U)], ACT.Copy).then_inc(s_idx, 1)

                if not deg:
                    @block.gpsimd
                    def _(pool):
                        with nc.gpsimd.Fori(0, groups // 2) as i:
                            for s in range(2):
                                pool.wait_ge(s_idx, i * 2 + s + 1)
                                pool.sem_inc(s_turn, 1)
                                for j in range(U):
                                    pool.indirect_dma_start(out=msg[:, s, j, :], out_offset=None, in_=table,
                                                            in_offset=bass.IndirectOffsetOnAxis(ap=idx[:, s, j:j + 1], axis=0)).then_inc(s_g[s], 16)

                def span(eng, g):
                    first = eng.value_load(spans[which][0:1, 0, bass.ds(g, 1)], min_val=0, max_val=NB - 1)
                    end = eng.value_load(spans[which][0:1, 1, bass.ds(g, 1)], min_val=1, max_val=NB)
                    return first, end

                def extra(eng, g):
                    return eng.value_load(spans[which][0:1, 2, bass.ds(g, 1)], min_val=0, max_val=NTILE * NB)

                @block.vector
                def _(v):
                    v.sem_inc(s_vec, 2)
                    v.sem_inc(s_rel[2], NB)
                    v.sem_inc(s_oh[2], NB)

                    def build(a, s, k, mine):
                        v.tensor_scalar(rel[:, k, :], cols[:, s, 0, :], base[:, bass.ds(a, 1)], None, ALU.subtract).then_inc(s_rel[k], 1)
                        v.wait_ge(s_rel[k], mine)
                        for j in range(U):
                            if deg:
                                last = v.tensor_scalar(oh[k][:, j, :], iotah[:, :], rel[:, k, j:j + 1], None, ALU.is_equal)
                            else:
                                last = v.tensor_scalar(oh[k][:, j, :], iota[:, :], rel[:, k, j:j + 1], cols[:, s, 1, j:j + 1], ALU.is_equal, ALU.mult)
                        last.then_inc(s_oh[k], 1)

                    with nc.vector.Fori(0, groups // 2) as i:
                        for s in range(2):
                            g = i * 2 + s
                            first, end = span(v, g)
                            v.wait_ge(s_cols, g + 1)
                            v.wait_ge(s_mm[s], i + 1)
                            build(first, s, s, i + 1)
                            with nc.vector.If(end > first + 1):
                                shift = extra(v, g)
                                with nc.vector.Fori(first + 1, end) as a:
                                    v.wait_ge(s_mm[2], shift + a)
                                    build(a, s, 2, shift + a)
                                    v.wait_ge(s_oh[2], shift + a)
                            v.sem_inc(s_seen, 1)
                            v.wait_ge(s_oh[s], i + 1)
                            v.sem_inc(s_vec, 1)

                @block.tensor
                def _(pe):
                    for a0 in range(0, NB, 512 // stride):
                        w = min(512, NB * stride - a0 * stride)
                        last = pe.matmul(sums[:, a0 * stride:a0 * stride + w], (identh if deg else ident)[:, :],
                                         self_rows[:, a0 * stride:a0 * stride + w],
                                         start=True, stop=True)
                    last.then_inc(s_init, 1)
                    pe.wait_ge(s_init, 1)
                    pe.sem_inc(s_pe, 2)
                    pe.sem_inc(s_mm[0], 1)
                    pe.sem_inc(s_mm[1], 1)
                    pe.sem_inc(s_mm[2], NB + 1)

                    def add(a, s, k):
                        n = 4 if deg else C
                        for j in range(U):
                            last = pe.matmul(sums[:, bass.ds(a * stride, n)], oh[k][:, j, :], msg[:, s, j, :], start=False, stop=True,
                                             skip_group_check=True)
                        last.then_inc(s_mm[k], 1)

                    with nc.tensor.Fori(0, groups // 2) as i:
                        for s in range(2):
                            g = i * 2 + s
                            first, end = span(pe, g)
                            if deg:
                                pe.wait_ge(s_idx, g + 1)
                            else:
                                pe.wait_ge(s_g[s], (i + 1) * (16 * U))
                            pe.sem_inc(s_rows, 1)
                            pe.wait_ge(s_oh[s], i + 1)
                            add(first, s, s)
                            with nc.tensor.If(end > first + 1):
                                shift = extra(pe, g)
                                with nc.tensor.Fori(first + 1, end) as a:
                                    pe.wait_ge(s_oh[2], shift + a)
                                    add(a, s, 2)
                                pe.wait_ge(s_mm[2], shift + end)
                                pe.sem_inc(s_rows, 1)
                            pe.wait_ge(s_mm[s], i + 2)
                            pe.sem_inc(s_pe, 1)

        def pow_phase(name, todo):
            with ExitStack() as c:
                s_a, s_b, s_c = sem(f"pa_{name}"), sem(f"pb_{name}"), sem(f"pc_{name}")
                block = c.enter_context(nc.Block())
                todo(block, s_a, s_b, s_c)

        def before_degrees(block, a, b, c_):
            @block.gpsimd
            def _(pool):
                pow_neg_half(pool, rstd[:, :], tmp[:, :]).then_inc(a, 1)
        pow_phase("ln1", before_degrees)
        edge_pass("deg", 4, 4, UD, None, bf16)

        def degrees(block, a, b, c_):
            @block.vector
            def _(v):
                v.tensor_reduce(dis[:, :], sums[:, 0:NB * 4].rearrange("p (b c) -> p b c", c=4), AX.X, ALU.add).then_inc(c_, 1)
                v.wait_ge(c_, 1)
                v.tensor_scalar(tmp[:, :], dis[:, :], 1e-12, None, ALU.max).then_inc(a, 1)
                v.wait_ge(a, 1)
                v.tensor_scalar(dis[:, :], dis[:, :], 0.0, None, ALU.is_gt).then_inc(c_, 1)
                v.wait_ge(b, 1)
                v.wait_ge(c_, 2)
                v.tensor_tensor(dis[:, :], dis[:, :], mv[:, :, 1], ALU.mult)

            @block.gpsimd
            def _(pool):
                pool.wait_ge(a, 1)
                pow_neg_half(pool, mv[:, :, 1], tmp[:, :]).then_inc(b, 1)
        pow_phase("deg", degrees)

        def normalise(block, name, s_extra=None):
            s_n, s_t, s_e = sem(f"normed_{name}"), sem(f"transposed_{name}"), sem(f"xT_{name}")

            @block.vector
            def _(v):
                with nc.vector.Fori(0, NT) as i:
                    for j in range(TS):
                        t = i * TS + j
                        v.wait_ge(s_t, t + 1)
                        v.tensor_scalar(xn[:, 0, :], xr[:, bass.ds(t, 1), :].rearrange("p a d -> p (a d)"),
                                        mv[:, bass.ds(t, 1), 0:1].rearrange("p a b -> p (a b)"),
                                        rstd[:, bass.ds(t, 1)], ALU.subtract, ALU.mult).then_inc(s_n, 1)

            @block.tensor
            def _(pe):
                pe.sem_inc(s_t, 1)
                with nc.tensor.Fori(0, NT) as i:
                    for j in range(TS):
                        t = i * TS + j
                        pe.wait_ge(s_n, t + 1)
                        pe.wait_ge(s_e, t + 1)
                        for k in range(KD):
                            last = pe.transpose(bank[0][:, k * P:(k + 1) * P], xn[:, 0, k * P:(k + 1) * P], ident[:, :])
                        last.then_inc(s_t, 1)

            @block.scalar
            def _(act):
                act.sem_inc(s_e, 1)
                with nc.scalar.Fori(0, NT) as i:
                    for j in range(TS):
                        t = i * TS + j
                        act.wait_ge(s_t, t + 2)
                        act.activation(xT[:, :, bass.ds(t * P, P)], bank[0][:, 0:KD * P].rearrange("p (k c) -> p k c", k=KD),
                                       ACT.Copy).then_inc(s_e, 1)

        with ExitStack() as c:
            block = c.enter_context(nc.Block())
            normalise(block, "ln1")

        def make_table(name, K, pieces, lhsT_of, w_tile, C, table):
            with ExitStack() as c:
                s_h, s_s, s_d = sem(f"rows_{name}"), sem(f"scaled_{name}"), sem(f"stored_{name}")
                block = c.enter_context(nc.Block())

                @block.tensor
                def _(pe):
                    for t in range(NB):
                        if t >= 2:
                            pe.wait_ge(s_s, t - 1)
                        for k in range(pieces):
                            last = pe.matmul(bank[t % 2][:, 0:C], lhsT_of(k, t), w_tile[0:K, k, :], start=(k == 0), stop=(k == pieces - 1))
                        last.then_inc(s_h, 1)

                @block.vector
                def _(v):
                    for t in range(NB):
                        v.wait_ge(s_h, t + 1)
                        v.tensor_scalar(acc[:, t * C:(t + 1) * C], bank[t % 2][:, 0:C], dis[:, t:t + 1], None, ALU.mult).then_inc(s_s, 1)

                @block.sync
                def _(sp):
                    sp.wait_ge(s_s, NB)
                    sp.dma_start(table.rearrange("(b p) c -> p b c", p=P), acc_of(C)).then_inc(s_d, 16)
                    sp.wait_ge(s_d, 16)

        with ExitStack() as cg:
            w1t = cg.enter_context(nc.sbuf_tensor("gw1_sb", [P, KD, H], f32))
            w2t = cg.enter_context(nc.sbuf_tensor("gw2_sb", [H, 1, L], f32))
            b1row = cg.enter_context(nc.sbuf_tensor("gb1_sb", [P, H], f32))
            b2row = cg.enter_context(nc.sbuf_tensor("gb2_sb", [P, L], f32))
            wd1t = cg.enter_context(nc.sbuf_tensor("wd1_sb", [L, H], f32))
            wd2t = cg.enter_context(nc.sbuf_tensor("wd2_sb", [H + 1, D], f32))
            bd1c = cg.enter_context(nc.sbuf_tensor("bd1_sb", [H, 1], f32))
            with ExitStack() as c:
                s_w = sem("gnn_weights_in")
                block = c.enter_context(nc.Block())

                @block.sync
                def _(sp):
                    sp.dma_start(w1t[:, :, :], gw1.rearrange("(k p) h -> p k h", p=P)).then_inc(s_w, 16)
                    sp.dma_start(w2t[:, 0, :], gw2).then_inc(s_w, 16)
                    sp.dma_start(b1row[:, :], gb1.rearrange("(o h) -> o h", o=1).broadcast_to([P, H])).then_inc(s_w, 16)
                    sp.dma_start(b2row[:, :], gb2.rearrange("(o h) -> o h", o=1).broadcast_to([P, L])).then_inc(s_w, 16)
                    sp.dma_start(wd1t[:, :], wd1).then_inc(s_w, 16)
                    sp.dma_start(wd2t[0:H, :], wd2).then_inc(s_w, 16)
                    sp.dma_start(wd2t[H:H + 1, :], bd2.rearrange("(o h) -> o h", o=1)).then_inc(s_w, 16)
                    sp.dma_start(bd1c[:, :], bd1.rearrange("(h o) -> h o", o=1)).then_inc(s_w, 16)
                    sp.wait_ge(s_w, 128)

            make_table("g1", P, KD, lambda k, t: xT[:, k, t * P:(t + 1) * P], w1t, H, g1_dram)
            edge_pass("c1", H, H, UC, g1_dram, f32)

            hT = xT[:, 0, :]

            def finish_conv(name, C, brow):
                with ExitStack() as c:
                    s_c, s_t, s_e = sem(f"relu_{name}"), sem(f"hT_psum_{name}"), sem(f"hT_{name}")
                    block = c.enter_context(nc.Block())

                    @block.vector
                    def _(v):
                        a = acc_of(C)
                        v.tensor_tensor(a, sums[:, 0:NB * C].rearrange("p (b c) -> p b c", c=C), dis[:, :].unsqueeze(2).broadcast_to([P, NB, C]), ALU.mult).then_inc(s_c, 1)
                        v.wait_ge(s_c, 1)
                        v.tensor_tensor(a, a, brow[:, :].unsqueeze(1).broadcast_to([P, NB, C]), ALU.add).then_inc(s_c, 1)
                        v.wait_ge(s_c, 2)
                        v.tensor_scalar(a, a, 0.0, None, ALU.max).then_inc(s_c, 1)

                    @block.tensor
                    def _(pe):
                        pe.wait_ge(s_c, 3)
                        for q, t0 in enumerate(range(0, NB, 4)):
                            if q >= 2:
                                pe.wait_ge(s_e, q - 1)
                            for t in range(t0, min(t0 + 4, NB)):
                                last = pe.transpose(bank[q % 2][0:C, (t - t0) * P:(t - t0 + 1) * P], acc[:, t * C:(t + 1) * C], ident[:, :])
                            last.then_inc(s_t, 1)

                    @block.scalar
                    def _(act):
                        for q, t0 in enumerate(range(0, NB, 4)):
                            w = min(4, NB - t0) * P
                            act.wait_ge(s_t, q + 1)
                            act.activation(hT[0:C, t0 * P:t0 * P + w], bank[q % 2][0:C, 0:w], ACT.Copy).then_inc(s_e, 1)

            finish_conv("c1", H, b1row)
            make_table("g2", H, 1, lambda k, t: hT[0:H, t * P:(t + 1) * P], w2t, L, g2_dram)
            edge_pass("c2", L, L, UC, g2_dram, f32)
            finish_conv("c2", L, b2row)

            with ExitStack() as c:
                s_d, s_dr, s_y, s_sg, s_x1, s_st = sem("d_psum"), sem("d_relu"), sem("xhat_psum"), sem("sigmoid"), sem("x1"), sem("stats2")
                s_one, s_pw = sem("ones_row"), sem("rstd2")
                sg = c.enter_context(nc.sbuf_tensor("sg", [P, 2, D], f32))
                block = c.enter_context(nc.Block())
                dT = xT[:, 1, :]
                NQ = -(-NP // 512)

                @block.tensor
                def _(pe):
                    for q in range(NQ):
                        w = min(512, NP - q * 512)
                        if q >= 2:
                            pe.wait_ge(s_dr, q - 1)
                        pe.matmul(bank[q % 2][0:H, 0:w], wd1t[:, :], hT[0:L, q * 512:q * 512 + w], start=True, stop=True).then_inc(s_d, 1)
                    pe.wait_ge(s_one, 1)
                    pe.wait_ge(s_dr, NQ)
                    for t in range(NB):
                        if t >= 2:
                            pe.wait_ge(s_sg, t - 1)
                        pe.matmul(bank[2 + t % 2][:, 0:D], dT[0:H + 1, t * P:(t + 1) * P], wd2t[:, :], start=True, stop=True).then_inc(s_y, 1)

                @block.scalar
                def _(act):
                    for q in range(NQ):
                        w = min(512, NP - q * 512)
                        act.wait_ge(s_d, q + 1)
                        act.activation(dT[0:H, q * 512:q * 512 + w], bank[q % 2][0:H, 0:w], ACT.Relu, bias=bd1c[:, :]).then_inc(s_dr, 1)
                    for t in range(NB):
                        act.wait_ge(s_y, t + 1)
                        if t >= 2:
                            act.wait_ge(s_x1, t - 1)
                        act.activation(sg[:, t % 2, :], bank[2 + t % 2][:, 0:D], ACT.Sigmoid).then_inc(s_sg, 1)

                @block.vector
                def _(v):
                    v.memset(dT[H:H + 1, :], 1.0).then_inc(s_one, 1)
                    for t in range(NB):
                        v.wait_ge(s_sg, t + 1)
                        v.tensor_tensor(xr[:, t, :], xr[:, t, :], sg[:, t % 2, :], ALU.add).then_inc(s_x1, 1)
                    v.wait_ge(s_x1, NB)
                    for t in range(NB):
                        last = v.bn_stats(stat[:, t, :], xr[:, t, :])
                    last.then_inc(s_st, 1)
                    v.wait_ge(s_st, 1)
                    for t in range(NB):
                        last = v.bn_aggr(mv[:, t, :], stat[:, t, :])
                    last.then_inc(s_st, 1)
                    v.wait_ge(s_st, 2)
                    v.tensor_scalar(tmp[:, :], mv[:, :, 1], EPS, None, ALU.add).then_inc(s_st, 1)

                @block.gpsimd
                def _(pool):
                    pool.wait_ge(s_st, 3)
                    pow_neg_half(pool, rstd[:, :], tmp[:, :]).then_inc(s_pw, 1)

        with ExitStack() as c:
            block = c.enter_context(nc.Block())
            normalise(block, "ln2")

        graph.close()

        with ExitStack() as c:
            def sbr(name, shape, dt=f32):
                return c.enter_context(nc.sbuf_tensor(name, shape, dt))
            wrt = sbr("wr_sb", [P, KD, NE])
            lg = sbr("lg", [P, NB, NE])
            m8 = sbr("m8", [P, NB, NE])
            i8 = sbr("i8", [P, NB, NE], u32)
            i8f = sbr("i8f", [P, NB, 2])
            dl = sbr("dl", [P, NB, 2])
            eq = sbr("eq", [P, 2, NB, NE])
            both = sbr("both", [P, NB, NE])
            slot = sbr("slot", [P, NB, NE])
            upto = sbr("upto", [P, NE, NB])
            prod = sbr("prod", [P, NB, NE])
            zer = sbr("zer_row", [P, NB])
            nu = sbr("nu", [P, NE])
            nui = sbr("nui", [P, NE], i32)
            uend = sbr("uend", [P, NE])
            ei = sbr("ei", [P, NE], i32)
            ef = sbr("ef", [P, NE])
            b1r = sbr("b1r", [(NE + 1) * KF, P])
            s_bt, s_both, s_cnt = sem("biases_transposed"), sem("choices"), sem("counts")
            s_w, s_l, s_i, s_ch, s_dl, s_wt = sem("wr_in"), sem("logits"), sem("expert_ids"), sem("routerchain"), sem("gap"), sem("topw_set")
            block = c.enter_context(nc.Block())

            @block.sync
            def _(sp):
                sp.dma_start(wrt[:, :, :], wr.rearrange("(k p) e -> p k e", p=P)).then_inc(s_w, 16)
                sp.dma_start(b1r[0:NE * KF, :], b1p.rearrange("e (k p) -> (e k) p", p=P)).then_inc(s_w, 16)
                sp.dma_start(b1r[NE * KF:(NE + 1) * KF, :], b1s.rearrange("(k p) -> k p", p=P)).then_inc(s_w, 16)

            @block.gpsimd
            def _(pool):
                pool.memset(zer[:, :], 0.0)
                pool.iota(ei[:, :], pattern=[[1, NE]], base=0, channel_multiplier=0).then_inc(s_i, 1)

            @block.tensor
            def _(pe):
                pe.wait_ge(s_w, 48)
                pe.transpose(bank[1][:, 0:(NE + 1) * KF], b1r[:, :], ident[0:(NE + 1) * KF, 0:(NE + 1) * KF]).then_inc(s_bt, 1)
                for t in range(NB):
                    for k in range(KD):
                        last = pe.matmul(bank[0][:, t * NE:(t + 1) * NE], xT[:, k, t * P:(t + 1) * P], wrt[:, k, :], start=(k == 0), stop=(k == KD - 1))
                last.then_inc(s_l, 1)
                pe.wait_ge(s_both, 1)
                pe.matmul(bank[2][:, 0:NB * NE], tri[:, :], both[:, :, :].rearrange("p b e -> p (b e)"), start=True, stop=True)
                pe.matmul(bank[3][:, 0:NB * NE], ones[:, :], both[:, :, :].rearrange("p b e -> p (b e)"), start=True, stop=True).then_inc(s_cnt, 1)

            @block.scalar
            def _(act):
                act.wait_ge(s_dl, 1)
                act.activation(topw[:, :, :], dl[:, :, :], ACT.Sigmoid).then_inc(s_wt, 1)

            @block.vector
            def _(v):
                n = [0]

                def link(ins):
                    n[0] += 1
                    ins.then_inc(s_ch, 1)
                    v.wait_ge(s_ch, n[0])
                v.wait_ge(s_bt, 1)
                v.tensor_copy(b1t[:, :], bank[1][:, 0:(NE + 1) * KF])
                v.wait_ge(s_l, 1)
                link(v.tensor_copy(lg[:, :, :], bank[0][:, 0:NB * NE].rearrange("p (t e) -> p t e", e=NE)))
                for t in range(NB):
                    last = v.max(m8[:, t, :], lg[:, t, :])
                link(last)
                for t in range(NB):
                    last = v.max_index(i8[:, t, :], m8[:, t, :], lg[:, t, :])
                link(last)
                link(v.tensor_copy(i8f[:, :, :], i8[:, :, 0:2]))
                link(v.tensor_tensor(dl[:, :, 0], m8[:, :, 0], m8[:, :, 1], ALU.subtract))
                v.tensor_tensor(dl[:, :, 1], m8[:, :, 1], m8[:, :, 0], ALU.subtract).then_inc(s_dl, 1)
                v.wait_ge(s_i, 1)
                link(v.tensor_copy(ef[:, :], ei[:, :]))
                for k in range(2):
                    last = v.tensor_tensor(eq[:, k, :, :], ef[:, :].unsqueeze(1).broadcast_to([P, NB, NE]), i8f[:, :, k:k + 1].broadcast_to([P, NB, NE]), ALU.is_equal)
                link(last)
                link(v.tensor_tensor(both[:, :, :], eq[:, 0, :, :], eq[:, 1, :, :], ALU.add))
                v.tensor_scalar(both[:, NB - 1, :], both[:, NB - 1, :], valid[:, :], None, ALU.mult).then_inc(s_both, 1)
                v.wait_ge(s_cnt, 1)
                count = bank[3][:, 0:NB * NE].rearrange("p (b e) -> p b e", e=NE)
                for e in range(NE):
                    last = v.tensor_tensor_scan(upto[:, e, :], count[:, :, e], zer[:, :], 0.0, ALU.add, ALU.add)
                link(last)
                link(v.tensor_scalar(nu[:, :], upto[:, :, NB - 1], 1.0, float(UT - 1), ALU.max, ALU.add))
                link(v.tensor_copy(nui[:, :], nu[:, :]))
                link(v.tensor_scalar(nui[:, :], nui[:, :], UT.bit_length() - 1, None, ALU.arith_shift_right))
                link(v.tensor_copy(nu[:, :], nui[:, :]))
                link(v.tensor_tensor_scan(uend[:, :], nu[:, :], zer[:, 0:NE], 0.0, ALU.add, ALU.add))
                link(v.tensor_copy(ends[:, :], uend[0:1, :]))
                link(v.tensor_tensor(nu[:, :], uend[:, :], nu[:, :], ALU.subtract))
                link(v.tensor_scalar(nu[:, :], nu[:, :], float(UT), None, ALU.mult))
                link(v.tensor_tensor(slot[:, :, :], upto[:, :, :].rearrange("p e b -> p b e"), count, ALU.subtract))
                link(v.tensor_tensor(slot[:, :, :], slot[:, :, :], bank[2][:, 0:NB * NE].rearrange("p (b e) -> p b e", e=NE), ALU.add))
                link(v.tensor_tensor(slot[:, :, :], slot[:, :, :], nu[:, :].unsqueeze(1).broadcast_to([P, NB, NE]), ALU.add))
                for k in range(2):
                    link(v.tensor_tensor(prod[:, :, :], slot[:, :, :], eq[:, k, :, :], ALU.mult))
                    link(v.tensor_reduce(slots[:, :, k], prod[:, :, :], AX.X, ALU.add))

        b1_of = lambda e, f: b1t[:, e * KF + f:e * KF + f + 1]
        hh = sb("hh", [P, KF, UT])
        w1s_t = sb("w1s_sb", [P, KD, F])
        w2s_t = sb("w2s_sb", [P, KF, D])
        b2s_t = sb("b2s_sb", [P, D])
        KH = KF // 2

        def up(pe, w1, rows_of, half_, W):
            for f in range(half_ * KH, (half_ + 1) * KH):
                for k in range(KD):
                    last = pe.matmul(bank[f // 2][:, (f % 2) * UT:(f % 2) * UT + W], w1[:, k, f * P:(f + 1) * P], rows_of(k),
                                     start=(k == 0), stop=(k == KD - 1))
            return last

        def down(pe, w2, half_, W):
            for h in range(W // P):
                for f in range(half_ * KH, (half_ + 1) * KH):
                    last = pe.matmul(bank[5 + h][:, 0:D], hh[:, f, h * P:(h + 1) * P], w2[:, f, :], start=(f == 0), stop=(f == KF - 1))
            return last

        def gelu(act, e, half_, W):
            for f in range(half_ * KH, (half_ + 1) * KH):
                last = act.activation(hh[:, f, 0:W], bank[f // 2][:, (f % 2) * UT:(f % 2) * UT + W], ACT.Gelu, bias=b1_of(e, f))
            return last

        TG = 4
        STEPS = (NB - 1) // TG
        PH = STEPS
        assert NB - 1 == TG * STEPS and 2 * PH * 2 == NB - 1

        class Shared:
            def __init__(self, name, t0, rest):
                self.t0, self.rest = t0, rest
                self.s_h, self.s_gl, self.s_y, self.s_yd, self.s_b = (sem(f"{w}_{name}") for w in ("h_psum", "gelu", "y_psum", "y_added", "bias_added"))

            def tensor(self, pe, u, t, W=UT):
                rows = lambda k: xT[:, k, bass.ds(t * P, W)]
                up(pe, w1s_t, rows, 0, W).then_inc(self.s_h, 1)
                up(pe, w1s_t, rows, 1, W).then_inc(self.s_h, 1)
                pe.wait_ge(self.s_yd, u + 1)
                pe.wait_ge(self.s_gl, u * 2 + 1)
                down(pe, w2s_t, 0, W)
                pe.wait_ge(self.s_gl, u * 2 + 2)
                down(pe, w2s_t, 1, W).then_inc(self.s_y, 1)

            def scalar(self, act, u, W=UT):
                for h in range(2):
                    act.wait_ge(self.s_h, u * 2 + h + 1)
                    gelu(act, NE, h, W).then_inc(self.s_gl, 1)

            def vector(self, v, u, t, W=UT):
                for h in range(W // P):
                    o = xr[:, bass.ds(t + h, 1), :].rearrange("p a d -> p (a d)")
                    last = v.tensor_tensor(o, o, b2s_t[:, :], ALU.add)
                last.then_inc(self.s_b, 1)
                v.wait_ge(self.s_b, u + 1)
                v.wait_ge(self.s_y, u + 1)
                for h in range(W // P):
                    o = xr[:, bass.ds(t + h, 1), :].rearrange("p a d -> p (a d)")
                    last = v.tensor_tensor(o, bank[5 + h][:, 0:D], o, ALU.add)
                last.then_inc(self.s_yd, 1)

            def tensor_program(self, pe):
                pe.sem_inc(self.s_yd, 1)
                with nc.tensor.Fori(0, PH) as i:
                    self.tensor(pe, i, i * 2 + self.t0)
                if self.rest:
                    self.tensor(pe, PH, NB - 1, P)

            def scalar_program(self, act):
                with nc.scalar.Fori(0, PH) as i:
                    self.scalar(act, i)
                if self.rest:
                    self.scalar(act, PH, P)

        with ExitStack() as c:
            xn4 = c.enter_context(nc.sbuf_tensor("xn4", [P, TG, D], f32))
            idx = c.enter_context(nc.sbuf_tensor("slot_of", [P, TG, 2], u32))
            zeros = c.enter_context(nc.sbuf_tensor("zeros", [P, 2, D], f32))
            s_ws, s_zs, s_z, s_zy, s_n, s_go = sem("shared_in"), sem("zeros_set"), sem("tails_zeroed"), sem("unused_zeroed"), sem("normed"), sem("scatter_started")
            s_sc = [sem(f"scattered{j}") for j in range(TG)]
            sh = Shared("shared1", 0, False)
            block = c.enter_context(nc.Block())

            @block.sync
            def _(sp):
                sp.dma_start(w1s_t[:, :, :], w1s.rearrange("(k p) f -> p k f", p=P)).then_inc(s_ws, 16)
                sp.dma_start(w2s_t[:, :, :], w2s.rearrange("(k p) d -> p k d", p=P)).then_inc(s_ws, 16)
                sp.dma_start(b2s_t[:, :], b2s.rearrange("(o d) -> o d", o=1).broadcast_to([P, D])).then_inc(s_ws, 16)
                sp.wait_ge(s_zs, 1)
                for e in range(NE):
                    end = sp.value_load(ends[0:1, e:e + 1], min_val=1, max_val=UMAX)
                    sp.dma_start(x_dram[bass.ds((end - 1) * UT, UT), :].rearrange("(h p) d -> p h d", p=P), zeros[:, :, :]).then_inc(s_z, 16)
                sp.dma_start(x_dram[bass.ds(end * UT, UT), :].rearrange("(h p) d -> p h d", p=P), zeros[:, :, :]).then_inc(s_z, 16)
                with nc.sync.Fori(end, UMAX + 1) as u:
                    sp.dma_start(y_dram[bass.ds(u * UT, UT), :].rearrange("(h p) d -> p h d", p=P), zeros[:, :, :]).then_inc(s_zy, 16)
                sp.wait_ge(s_z, 16 * (NE + 1))
                with nc.sync.Fori(0, end) as u:
                    sp.sem_inc(s_zy, 16)
                sp.wait_ge(s_zy, (UMAX + 1) * 16)

            @block.tensor
            def _(pe):
                pe.wait_ge(s_ws, 48)
                sh.tensor_program(pe)

            @block.scalar
            def _(act):
                sh.scalar_program(act)

            @block.vector
            def _(v):
                v.memset(zeros[:, :, :], 0.0).then_inc(s_zs, 1)
                def prepare(i, j, t):
                    if not isinstance(i, int) or i > 0:
                        v.wait_ge(s_sc[j], i * 32)
                    v.tensor_copy(idx[:, j, :], slots[:, bass.ds(t, 1), :].rearrange("p a k -> p (a k)"))
                    v.tensor_scalar(xn4[:, j, :], xr[:, bass.ds(t, 1), :].rearrange("p a d -> p (a d)"),
                                    mv[:, bass.ds(t, 1), 0:1].rearrange("p a b -> p (a b)"),
                                    rstd[:, bass.ds(t, 1)], ALU.subtract, ALU.mult).then_inc(s_n, 1)
                for j in range(TG):
                    prepare(0, j, j)
                with nc.vector.Fori(0, STEPS - 1) as i:
                    for j in range(TG):
                        prepare(i + 1, j, i * TG + TG + j)
                    sh.vector(v, i, i * 2)
                prepare(STEPS, 0, NB - 1)
                sh.vector(v, STEPS - 1, STEPS * 2 - 2)

            @block.gpsimd
            def _(pool):
                pool.wait_ge(s_z, 16 * (NE + 1))

                def scatter(n, j, rows):
                    pool.wait_ge(s_n, n + 1)
                    pool.sem_inc(s_go, 1)
                    for k in range(2):
                        pool.indirect_dma_start(out=x_dram, out_offset=bass.IndirectOffsetOnAxis(ap=idx[0:rows, j, k:k + 1], axis=0),
                                                in_=xn4[0:rows, j, :], in_offset=None).then_inc(s_sc[j], 16)
                with nc.gpsimd.Fori(0, STEPS) as i:
                    for j in range(TG):
                        scatter(i * TG + j, j, P)
                scatter(NB - 1, 0, LASTB)
                for j in range(TG):
                    pool.wait_ge(s_sc[j], 32 * (STEPS + (j == 0)))

        with ExitStack() as c:
            w1t = c.enter_context(nc.sbuf_tensor("w1_sb", [P, 2, KD, F], f32))
            w2t = c.enter_context(nc.sbuf_tensor("w2_sb", [P, 2, KF, D], f32))
            b2t = c.enter_context(nc.sbuf_tensor("b2_sb", [P, 2, D], f32))
            xin = c.enter_context(nc.sbuf_tensor("xin", [P, 2, D], f32))
            xu = c.enter_context(nc.sbuf_tensor("xu", [P, KD, UT], f32))
            ysb = c.enter_context(nc.sbuf_tensor("ysb", [P, 2, D], f32))
            s_w = [sem(f"expert_in{k}") for k in range(2)]
            s_xin, s_t, s_xu, s_h, s_gl, s_y, s_ysb, s_st = (sem(w) for w in (
                "unit_in", "unit_transposed", "unit_ready", "unit_h", "unit_gelu", "unit_y", "unit_result", "unit_stored"))
            s_tok = sem("expert_done")
            block = c.enter_context(nc.Block())

            def expert_end(eng, e):
                return eng.value_load(ends[0:1, e:e + 1], min_val=1, max_val=UMAX)

            def unit(table, u):
                return table[bass.ds(u * UT, UT), :].rearrange("(h p) d -> p h d", p=P)

            @block.gpsimd
            def _(pool):
                for e in range(NE):
                    if e >= 2:
                        pool.wait_ge(s_ysb, expert_end(pool, e - 2) + 1)
                        pool.sem_inc(s_tok, 1)
                    pool.dma_start(w1t[:, e % 2, :, :], w1p[e].rearrange("(k p) f -> p k f", p=P)).then_inc(s_w[e % 2], 16)
                    pool.dma_start(w2t[:, e % 2, :, :], w2p[e].rearrange("(k p) d -> p k d", p=P)).then_inc(s_w[e % 2], 16)
                    pool.dma_start(b2t[:, e % 2, :], b2p[e].rearrange("(o d) -> o d", o=1).broadcast_to([P, D])).then_inc(s_w[e % 2], 16)

            @block.sync
            def _(sp):
                sp.dma_start(xin[:, :, :], unit(x_dram, 0)).then_inc(s_xin, 16)
                total = expert_end(sp, NE - 1)
                with nc.sync.Fori(0, total) as u:
                    sp.wait_ge(s_t, u + 1)
                    sp.dma_start(xin[:, :, :], unit(x_dram, u + 1)).then_inc(s_xin, 16)
                    sp.wait_ge(s_ysb, u + 2)
                    sp.dma_start(unit(y_dram, u), ysb[:, :, :]).then_inc(s_st, 16)
                sp.wait_ge(s_st, total * 16 + 16)
                sp.sem_inc(s_tok, 1)

            @block.tensor
            def _(pe):
                pe.sem_inc(s_ysb, 1)

                def transposes(n):
                    pe.wait_ge(s_xin, n * 16 + 16)
                    for h in range(2):
                        for k in range(KD):
                            last = pe.transpose(bank[4][:, k * UT + h * P:k * UT + (h + 1) * P], xin[:, h, k * P:(k + 1) * P], ident[:, :])
                    last.then_inc(s_t, 1)
                transposes(0)
                first = 0
                for e in range(NE):
                    s = e % 2
                    end = expert_end(pe, e)
                    pe.wait_ge(s_w[s], 48 * (e // 2 + 1))
                    with nc.tensor.Fori(first, end) as u:
                        pe.wait_ge(s_xu, u + 1)
                        up(pe, w1t[:, s, :, :], lambda k: xu[:, k, :], 0, UT).then_inc(s_h, 1)
                        up(pe, w1t[:, s, :, :], lambda k: xu[:, k, :], 1, UT).then_inc(s_h, 1)
                        transposes(u + 1)
                        pe.wait_ge(s_ysb, u + 1)
                        pe.wait_ge(s_gl, u * 2 + 1)
                        down(pe, w2t[:, s, :, :], 0, UT)
                        pe.wait_ge(s_gl, u * 2 + 2)
                        down(pe, w2t[:, s, :, :], 1, UT).then_inc(s_y, 1)
                    first = end

            @block.scalar
            def _(act):
                first = 0
                for e in range(NE):
                    end = expert_end(act, e)
                    with nc.scalar.Fori(first, end) as u:
                        for h in range(2):
                            act.wait_ge(s_h, u * 2 + h + 1)
                            gelu(act, e, h, UT).then_inc(s_gl, 1)
                    first = end

            @block.vector
            def _(v):
                v.sem_inc(s_st, 16)

                def take(n):
                    v.wait_ge(s_t, n + 1)
                    v.tensor_copy(xu[:, :, :], bank[4][:, 0:KD * UT].rearrange("p (k c) -> p k c", k=KD)).then_inc(s_xu, 1)
                take(0)
                first = 0
                for e in range(NE):
                    end = expert_end(v, e)
                    with nc.vector.Fori(first, end) as u:
                        take(u + 1)
                        v.wait_ge(s_st, u * 16 + 16)
                        v.wait_ge(s_y, u + 1)
                        for h in range(2):
                            last = v.tensor_tensor(ysb[:, h, :], bank[5 + h][:, 0:D], b2t[:, e % 2, :], ALU.add)
                        last.then_inc(s_ysb, 1)
                    first = end

        with ExitStack() as c:
            got = c.enter_context(nc.sbuf_tensor("got", [P, TG, 2, D], f32))
            idx = c.enter_context(nc.sbuf_tensor("result_of", [P, TG, 2], u32))
            s_ix, s_cm, s_go, s_sv = sem("result_slots"), sem("combined"), sem("gather_started"), sem("out_stored")
            s_g = [sem(f"results_in{j}") for j in range(TG)]
            sh = Shared("shared2", PH * 2, True)
            block = c.enter_context(nc.Block())

            @block.tensor
            def _(pe):
                sh.tensor_program(pe)

            @block.scalar
            def _(act):
                sh.scalar_program(act)

            @block.gpsimd
            def _(pool):
                def gather(n, j, rows):
                    pool.wait_ge(s_ix, n + 1)
                    pool.sem_inc(s_go, 1)
                    for k in range(2):
                        pool.indirect_dma_start(out=got[0:rows, j, k, :], out_offset=None, in_=y_dram,
                                                in_offset=bass.IndirectOffsetOnAxis(ap=idx[0:rows, j, k:k + 1], axis=0)).then_inc(s_g[j], 16)
                with nc.gpsimd.Fori(0, STEPS) as i:
                    for j in range(TG):
                        gather(i * TG + j, j, P)
                gather(NB - 1, 0, LASTB)

            @block.vector
            def _(v):
                def request(t, j):
                    v.tensor_copy(idx[:, j, :], slots[:, bass.ds(t, 1), :].rearrange("p a k -> p (a k)")).then_inc(s_ix, 1)

                def combine(i, j, t, rows=P, more=None):
                    v.wait_ge(s_g[j], i * 32 + 32)
                    o = xr[0:rows, bass.ds(t, 1), :].rearrange("p a d -> p (a d)")
                    for k in range(2):
                        w = topw[0:rows, bass.ds(t, 1), k:k + 1].rearrange("p a b -> p (a b)")
                        v.scalar_tensor_tensor(out=o, in0=got[0:rows, j, k, :], scalar=w, in1=o, op0=ALU.mult, op1=ALU.add).then_inc(s_cm, 1)
                        v.wait_ge(s_cm, t * 2 + k + 1)
                for j in range(TG):
                    request(j, j)
                with nc.vector.Fori(0, STEPS - 1) as i:
                    sh.vector(v, i, i * 2 + PH * 2)
                    for j in range(TG):
                        combine(i, j, i * TG + j)
                        request(i * TG + TG + j, j)
                sh.vector(v, STEPS - 1, STEPS * 2 - 2 + PH * 2)
                v.wait_ge(sh.s_yd, STEPS + 1)
                for j in range(TG):
                    combine(STEPS - 1, j, (STEPS - 1) * TG + j)
                    if j == 0:
                        request(NB - 1, 0)
                sh.vector(v, STEPS, NB - 1, P)
                v.wait_ge(sh.s_yd, STEPS + 2)
                combine(STEPS, 0, NB - 1, LASTB)

            @block.sync
            def _(sp):
                with nc.sync.Fori(0, STEPS) as i:
                    sp.wait_ge(s_cm, i * (2 * TG) + 2 * TG)
                    sp.dma_start(out[bass.ds(i * (TG * P), TG * P), :].rearrange("(b p) d -> p b d", p=P),
                                 xr[:, bass.ds(i * TG, TG), :]).then_inc(s_sv, 16)
                sp.wait_ge(s_cm, 2 * NB)
                sp.dma_start(out[(NB - 1) * P:N, :], xr[0:LASTB, NB - 1, :]).then_inc(s_sv, 16)
                sp.wait_ge(s_sv, 16 * (STEPS + 1))


_INS = ['x', 'src', 'dst', 'edge_weight', 'L0_gnn_W1', 'L0_gnn_b1', 'L0_gnn_W2', 'L0_gnn_b2', 'L0_gnn_Wd1', 'L0_gnn_bd1',
        'L0_gnn_Wd2', 'L0_gnn_bd2', 'L0_ffn_Wr', 'L0_ffn_W1s', 'L0_ffn_b1s', 'L0_ffn_W2s', 'L0_ffn_b2s', 'L0_ffn_W1p',
        'L0_ffn_b1p', 'L0_ffn_W2p', 'L0_ffn_b2p']


def kernel(**inputs):
    import numpy as _np
    import concourse.bacc as _bacc
    from concourse import mybir as _mybir
    from concourse.bass_utils import run_bass_kernel_spmd as _run

    nc = _bacc.Bacc("TRN2", target_bir_lowering=False, num_devices=1)
    arrays, args = {}, []
    for name in _INS:
        a = _np.ascontiguousarray(inputs[name])
        arrays[f"in_{name}_dram"] = a
        args.append(nc.dram_tensor(f"in_{name}_dram", a.shape, _mybir.dt.from_np(a.dtype), kind="ExternalInput").ap())
    shape = inputs['x'].shape
    args.append(nc.dram_tensor("out_0_dram", tuple(shape), _mybir.dt.float32, kind="ExternalOutput").ap())
    gnn_moe_kernel(nc, *args)
    r = _run(nc, [arrays], core_ids=[0])
    return r.results[0]["out_0_dram"]
```

```python
import concourse.bass as bass
from concourse import mybir
from contextlib import ExitStack


def gnn_moe_kernel(nc, x, src, dst, ew, gw1, gb1, gw2, gb2, wd1, bd1, wd2, bd2,
                   wr, w1s, b1s, w2s, b2s, w1p, b1p, w2p, b2p, out):
    f32, i32, u32, f32r = mybir.dt.float32, mybir.dt.int32, mybir.dt.uint32, mybir.dt.float32r
    ALU, ACT, AX = mybir.AluOpType, mybir.ActivationFunctionType, mybir.AxisListType
    P = 128
    N, D = x.shape
    E = src.shape[0]
    H, L = gw2.shape
    NE = wr.shape[1]
    F = w1s.shape[1]
    KD, KF = D // P, F // P
    NB = -(-N // P)
    NP = NB * P
    LASTB = N - (NB - 1) * P
    UC, UD = 8, 16
    UA = 2
    P2 = P // 2
    NH = NP // P2
    NTILE = -(-E // (P * 2 * UD)) * 2 * UD
    RB = -(-NTILE // P)
    NG = NTILE // UC
    assert NTILE % (4 * UC) == 0 and NTILE == 2 * UD * NB
    FULL = E // P
    REST = E - FULL * P
    TS = 7
    NT = NB // TS
    assert NB == NT * TS and NE == 8
    EPS = 1e-5

    g1_dram = nc.dram_tensor("g1_table", (NP, H), f32).ap()
    g2_dram = nc.dram_tensor("g2_table", (NP, L), f32).ap()
    span_dram = nc.dram_tensor("span_scratch", (2, RB * P // UC), i32).ap()
    UT = 2 * P
    UMAX = N * 2 // UT + NE
    x_dram = nc.dram_tensor("expert_rows", ((UMAX + 1) * UT, D), f32).ap()
    y_dram = nc.dram_tensor("expert_results", ((UMAX + 1) * UT, D), f32).ap()

    with ExitStack() as ctx:
        graph = ExitStack()

        def sb(name, shape, dt=f32):
            return ctx.enter_context(nc.sbuf_tensor(name, shape, dt))

        def sbg(name, shape, dt=f32):
            return graph.enter_context(nc.sbuf_tensor(name, shape, dt))

        def sem(name):
            return ctx.enter_context(nc.semaphore(name))

        s_mark = sem("marks")
        sums = ctx.enter_context(nc.psum_tensor("psum", [P, 8 * 512], f32))
        bank = [sums[:, i * 512:(i + 1) * 512] for i in range(8)]

        xr = sb("xr", [P, NB, D])
        tri = sb("tri", [P, P])
        ones = sb("ones", [P, P])
        ident = sb("ident", [P, P])
        valid = sb("valid", [P, 1])
        mv = sb("mv", [P, NB, 2])
        rstd = sb("rstd", [P, NB])
        b1t = sb("b1t", [P, (NE + 1) * KF])
        topw = sb("topw", [P, NB, 2])
        slots = sb("slots", [P, NB, 2])
        ends = sb("ends", [1, NE], i32)
        raw1 = sb("raw1", [P, KD, F])
        raw2 = sb("raw2", [P, KF, D])
        normal = ExitStack()
        xT = normal.enter_context(nc.sbuf_tensor("xT", [P, KD, NP], f32))
        edges = sbg("edges", [P, 3, RB * P])
        iota = sbg("iota", [P, P])
        base = sbg("base", [P, NB])
        acc = sbg("acc", [P, NB * H])

        def acc_of(C):
            return acc[:, 0:NB * C].rearrange("p (b c) -> p b c", c=C)
        dis = sbg("dis", [P, NB])
        stat = sbg("stat", [P, NB, 6])
        tmp = sbg("tmp", [P, NB])
        half = sbg("half", [P, NB])
        spans = sbg("spans", [1, 3, NG], i32)
        nmr = sbg("nmr", [P, NB])
        xn = sbg("xn", [P, 2, D])
        gw1_t = sbg("gw1_sb", [P, KD, H])
        gw2_t = sbg("gw2_sb", [H, 1, L])
        b1row = sbg("gb1_sb", [P, H])
        b2row = sbg("gb2_sb", [P, L])
        wd1t = sbg("wd1_sb", [L, H])
        wd2t = sbg("wd2_sb", [H + 1, D])
        bd1c = sbg("bd1_sb", [H, 1])
        dst_low, dst_high, dst_neg = (xT[:, 0, k * NTILE:(k + 1) * NTILE] for k in range(3))

        def load_raw(eng, a, b, s):
            eng.dma_start(raw1[:, :, :], a.rearrange("(k p) f -> p k f", p=P)).then_inc(s, 16)
            eng.dma_start(raw2[:, :, :], b.rearrange("(k p) d -> p k d", p=P)).then_inc(s, 16)

        s_raw, s_split_u, s_split = sem("raw_in"), sem("weights_upper"), sem("weights_split")

        def pow_neg_half(pool, out_, in_):
            return nc.gpsimd.tensor_tensor(out_, in_, half[:, :], ALU.pow)

        with ExitStack() as c1:
            rows = [c1.enter_context(nc.sbuf_tensor(f"rows{k}", [P, RB, P], f32)) for k in range(3)]
            irow = c1.enter_context(nc.sbuf_tensor("irow", [P, RB, P], i32))
            mm = c1.enter_context(nc.sbuf_tensor("mm", [P, 2, RB], f32))
            mmg = c1.enter_context(nc.sbuf_tensor("mmg", [RB, 2, P // UC], f32))
            mmi = c1.enter_context(nc.sbuf_tensor("mmi", [RB, 2, P // UC], i32))
            q4 = c1.enter_context(nc.sbuf_tensor("q4", [1, 2, RB * P // UC], i32))
            q4f = c1.enter_context(nc.sbuf_tensor("q4f", [1, 2, NG], f32))
            nvf = c1.enter_context(nc.sbuf_tensor("nvf", [1, 2, NG], f32))
            dsti = c1.enter_context(nc.sbuf_tensor("dsti", [P, NTILE], i32))
            iotai = c1.enter_context(nc.sbuf_tensor("iotai", [P, P + NB], i32))
            zer = c1.enter_context(nc.sbuf_tensor("zer", [1, NG], f32))
            s_pad, s_src, s_dst, s_ew = sem("pad_set"), sem("src_in"), sem("dst_in"), sem("ew_in")
            s_xb, s_w, s_var, s_r = sem("x_rest_in"), sem("gnn_weights_in"), sem("variance"), sem("rstd1")
            s_x, s_xpad, s_conv, s_id = sem("x_in"), sem("xpad_set"), sem("rows_ready"), sem("consts_set")
            s_tp, s_ev, s_mm, s_mmt = sem("edges_transposed"), sem("edges_copied"), sem("minmax_ready"), sem("minmax_transposed")
            s_blk, s_sd, s_sl, s_ch, s_ch2, s_srcc = sem("blocks_ready"), sem("span_stored"), sem("span_loaded"), sem("vchain"), sem("pchain"), sem("src_used")
            block = c1.enter_context(nc.Block())
            RBF = FULL // P
            RR = FULL - RBF * P
            xb = x[0:(NB - 1) * P, :].rearrange("(b p) d -> p b d", p=P)

            @block.sync
            def _(sp):
                def load(dst_t, src_d, s):
                    sp.dma_start(dst_t[:, 0:RBF, :], src_d[0:RBF * P * P].rearrange("(b p j) -> p b j", p=P, j=P)).then_inc(s, 16)
                    sp.dma_start(dst_t[0:RR, RBF, :], src_d[RBF * P * P:FULL * P].rearrange("(p j) -> p j", j=P)).then_inc(s, 16)
                    sp.dma_start(dst_t[RR:RR + 1, RBF, 0:REST], src_d[FULL * P:E].rearrange("(p j) -> p j", p=1)).then_inc(s, 16)
                sp.wait_ge(s_pad, 1)
                load(irow, dst, s_dst)
                sp.wait_ge(s_pad, 2)
                load(rows[2], ew, s_ew)
                sp.wait_ge(s_srcc, 1)
                load(irow, src, s_src)
                sp.wait_ge(s_blk, 1)
                for m in range(2):
                    sp.dma_start(span_dram[m, :].rearrange("(b k) -> b k", b=RB), mmi[:, m, :]).then_inc(s_sd, 16)
                sp.wait_ge(s_sd, 32)
                sp.dma_start(q4[:, :, :], span_dram.rearrange("(o m) g -> o m g", o=1)).then_inc(s_sl, 16)
                sp.dma_start(gw1_t[:, :, :], gw1.rearrange("(k p) h -> p k h", p=P)).then_inc(s_w, 16)
                sp.dma_start(gw2_t[:, 0, :], gw2).then_inc(s_w, 16)
                sp.dma_start(b1row[:, :], gb1.rearrange("(o h) -> o h", o=1).broadcast_to([P, H])).then_inc(s_w, 16)
                sp.dma_start(b2row[:, :], gb2.rearrange("(o h) -> o h", o=1).broadcast_to([P, L])).then_inc(s_w, 16)
                sp.dma_start(wd1t[:, :], wd1).then_inc(s_w, 16)
                sp.dma_start(wd2t[0:H, :], wd2).then_inc(s_w, 16)
                sp.dma_start(wd2t[H:H + 1, :], bd2.rearrange("(o h) -> o h", o=1)).then_inc(s_w, 16)
                sp.dma_start(bd1c[:, :], bd1.rearrange("(h o) -> h o", o=1)).then_inc(s_w, 16)
                sp.wait_ge(s_sl, 16)
                sp.wait_ge(s_w, 128)

            XA = (NB - 1) // 2

            @block.scalar
            def _(act):
                act.wait_ge(s_xpad, 1)
                act.wait_ge(s_src, 48)
                act.dma_start(xr[:, 0:XA, :], xb[:, 0:XA, :]).then_inc(s_x, 16)
                act.dma_start(xr[:, XA:NB - 1, :], xb[:, XA:NB - 1, :]).then_inc(s_xb, 16)
                act.dma_start(xr[0:LASTB, NB - 1, :], x[(NB - 1) * P:N, :]).then_inc(s_xb, 16)

            @block.gpsimd
            def _(pool):
                pool.memset(ident[:, :], 0.0)
                pool.memset(ones[:, :], 1.0)
                pool.memset(half[:, :], -0.5)
                pool.memset(zer[:, :], 0.0)
                pool.memset(tri[:, :], 1.0)
                pool.memset(valid[:, :], 1.0)
                pool.iota(iotai[:, 0:P], pattern=[[1, P]], base=0, channel_multiplier=0)
                pool.iota(iotai[:, P:P + NB], pattern=[[P, NB]], base=0, channel_multiplier=0).then_inc(s_ch2, 1)
                pool.wait_ge(s_ch2, 1)
                pool.affine_select(out=tri[:, :], in_=tri[:, :], compare_op=ALU.is_gt, fill=0.0,
                                   base=0, pattern=[[1, P]], channel_multiplier=-1)
                pool.affine_select(out=valid[:, :], in_=valid[:, :], compare_op=ALU.is_ge, fill=0.0,
                                   base=LASTB - 1, pattern=[[0, 1]], channel_multiplier=-1)
                pool.affine_select(out=ident[:, :], in_=ident[:, :], compare_op=ALU.not_equal, fill=1.0,
                                   base=0, pattern=[[-1, P]], channel_multiplier=1).then_inc(s_id, 1)
                pool.wait_ge(s_var, 1)
                pow_neg_half(pool, rstd[:, :], tmp[:, :]).then_inc(s_r, 1)

            @block.vector
            def _(v):
                n = [0]

                def link(ins):
                    n[0] += 1
                    ins.then_inc(s_ch, 1)
                    v.wait_ge(s_ch, n[0])
                v.memset(xr[:, NB - 1, :], 0.0).then_inc(s_xpad, 1)
                v.memset(irow[:, RBF, :], N - 1).then_inc(s_pad, 1)
                v.memset(rows[2][:, RBF, :], 0.0).then_inc(s_pad, 1)
                v.wait_ge(s_dst, 48)
                link(v.tensor_copy(rows[1][:, :, :], irow[:, :, :]))
                v.memset(irow[:, RBF, :], 0).then_inc(s_srcc, 1)
                v.tensor_reduce(mm[:, 0, :], rows[1][:, :, :], AX.X, ALU.min)
                v.tensor_reduce(mm[:, 1, :], rows[1][:, :, :], AX.X, ALU.max).then_inc(s_mm, 1)
                v.wait_ge(s_ew, 48)
                v.wait_ge(s_src, 48)
                v.tensor_copy(rows[0][:, :, :], irow[:, :, :]).then_inc(s_conv, 1)
                v.wait_ge(s_mmt, 1)
                link(v.tensor_reduce(mmg[:, 0, :], bank[0][0:RB, 0:P].rearrange("p (g u) -> p g u", u=UC), AX.X, ALU.min))
                link(v.tensor_reduce(mmg[:, 1, :], bank[0][0:RB, P:2 * P].rearrange("p (g u) -> p g u", u=UC), AX.X, ALU.max))
                link(v.tensor_copy(mmi[:, :, :], mmg[:, :, :]))
                v.tensor_scalar(mmi[:, :, :], mmi[:, :, :], 7, None, ALU.arith_shift_right).then_inc(s_blk, 1)
                k = 0
                for b0 in range(0, RB, 4):
                    for a in range(3):
                        k += 1
                        v.wait_ge(s_tp, k)
                        w = min(4, RB - b0) * P
                        v.tensor_copy(edges[:, a, b0 * P:b0 * P + w], bank[1 + (k - 1) % 4][:, 0:w]).then_inc(s_ev, 1)
                v.wait_ge(s_x, 16)
                for t in range(XA):
                    v.bn_stats(stat[:, t, :], xr[:, t, :])
                v.wait_ge(s_xb, 32)
                for t in range(XA, NB):
                    last = v.bn_stats(stat[:, t, :], xr[:, t, :])
                link(last)
                for t in range(NB):
                    last = v.bn_aggr(mv[:, t, :], stat[:, t, :])
                link(last)
                v.tensor_scalar(tmp[:, :], mv[:, :, 1], EPS, None, ALU.add).then_inc(s_var, 1)
                v.wait_ge(s_sl, 16)
                link(v.tensor_copy(q4f[:, :, :], q4[:, :, 0:NG]))
                v.wait_ge(s_id, 1)
                before, more = nvf[:, 0, :], nvf[:, 1, :]
                first, last = q4f[:, 0, :], q4f[:, 1, :]
                link(v.tensor_copy(spans[:, 0, :], first))
                link(v.tensor_scalar(spans[:, 1, :], last, 1.0, None, ALU.add))
                link(v.tensor_tensor(more, last, first, ALU.subtract))
                link(v.tensor_tensor_scan(before, more, zer[:, :], 0.0, ALU.add, ALU.add))
                link(v.tensor_tensor(before, before, more, ALU.subtract))
                link(v.tensor_tensor(before, before, first, ALU.subtract))
                link(v.tensor_scalar(spans[:, 2, :], before, float(NB), None, ALU.add))
                d = edges[:, 1, 0:NTILE]
                link(v.tensor_copy(dsti[:, :], d))
                link(v.tensor_scalar(dsti[:, :], dsti[:, :], P2.bit_length() - 1, None, ALU.arith_shift_right))
                link(v.tensor_copy(dst_high, dsti[:, :]))
                v.scalar_tensor_tensor(out=dst_low, in0=dst_high, scalar=float(-P2), in1=d, op0=ALU.mult, op1=ALU.add)
                v.tensor_scalar(dst_neg, dst_high, -1.0, None, ALU.mult)
                v.tensor_copy(iota[:, :], iotai[:, 0:P])
                v.tensor_copy(base[:, :], iotai[:, P:P + NB])
                v.wait_ge(s_r, 1)
                v.scalar_tensor_tensor(out=nmr[:, :], in0=mv[:, :, 0], scalar=-1.0, in1=rstd[:, :], op0=ALU.mult, op1=ALU.mult)

            @block.tensor
            def _(pe):
                pe.wait_ge(s_id, 1)
                pe.wait_ge(s_mm, 1)
                pe.transpose(bank[0][0:RB, 0:P], mm[:, 0, :], ident[:, :])
                pe.transpose(bank[0][0:RB, P:2 * P], mm[:, 1, :], ident[:, :]).then_inc(s_mmt, 1)
                pe.wait_ge(s_conv, 1)
                k = 0
                for b0 in range(0, RB, 4):
                    for a in range(3):
                        k += 1
                        if k > 4:
                            pe.wait_ge(s_ev, k - 4)
                        for b in range(b0, min(b0 + 4, RB)):
                            last = pe.transpose(bank[1 + (k - 1) % 4][:, (b - b0) * P:(b - b0 + 1) * P], rows[a][:, b, :], ident[:, :])
                        last.then_inc(s_tp, 1)

        def edge_pass(name, C, table):
            U = UC
            groups = NG
            with ExitStack() as c:
                oh = [c.enter_context(nc.sbuf_tensor(f"oh{k}_{name}", [P, U, P], f32)) for k in range(3)]
                rel = c.enter_context(nc.sbuf_tensor(f"rel_{name}", [P, 3, U], f32))
                cols = c.enter_context(nc.sbuf_tensor(f"cols_{name}", [P, 2, 2, U], f32))
                idx = c.enter_context(nc.sbuf_tensor(f"idx_{name}", [P, 4, U], u32))
                msg = c.enter_context(nc.sbuf_tensor(f"msg_{name}", [P, 4, U, C], f32))
                s_rel, s_oh, s_mm = ([sem(f"{w}{k}_{name}") for k in range(3)] for w in ("relative", "onehots", "summed"))
                s_idx, s_cols, s_init = sem(f"idx_{name}"), sem(f"cols_{name}"), sem(f"sums_started_{name}")
                s_g = [sem(f"gathered{k}_{name}") for k in range(4)]
                s_vec, s_pe = sem(f"cols_used_{name}"), sem(f"rows_used_{name}")
                block = c.enter_context(nc.Block())

                @block.scalar
                def _(act):
                    with nc.scalar.Fori(0, groups // 4) as i:
                        for n in range(4):
                            g = i * 4 + n
                            act.wait_ge(s_pe, g + 1)
                            act.activation(idx[:, n, :], edges[:, 0, bass.ds(g * U, U)], ACT.Copy).then_inc(s_idx, 1)
                            act.wait_ge(s_vec, g + 1)
                            act.activation(cols[:, n % 2, :, :], edges[:, 1:3, bass.ds(g * U, U)], ACT.Copy).then_inc(s_cols, 1)

                @block.gpsimd
                def _(pool):
                    with nc.gpsimd.Fori(0, groups // 4) as i:
                        for n in range(4):
                            pool.wait_ge(s_idx, i * 4 + n + 1)
                            pool.sem_inc(s_mark, 1)
                            for j in range(U):
                                pool.indirect_dma_start(out=msg[:, n, j, :], out_offset=None, in_=table,
                                                        in_offset=bass.IndirectOffsetOnAxis(ap=idx[:, n, j:j + 1], axis=0)).then_inc(s_g[n], 16)

                def span(eng, g):
                    first = eng.value_load(spans[0:1, 0, bass.ds(g, 1)], min_val=0, max_val=NB - 1)
                    end = eng.value_load(spans[0:1, 1, bass.ds(g, 1)], min_val=1, max_val=NB)
                    return first, end

                def extra(eng, g):
                    return eng.value_load(spans[0:1, 2, bass.ds(g, 1)], min_val=0, max_val=NTILE * NB)

                @block.vector
                def _(v):
                    v.sem_inc(s_vec, 2)
                    v.sem_inc(s_rel[2], NB)
                    v.sem_inc(s_oh[2], NB)

                    def build(a, s, k, mine):
                        v.tensor_scalar(rel[:, k, :], cols[:, s, 0, :], base[:, bass.ds(a, 1)], None, ALU.subtract).then_inc(s_rel[k], 1)
                        v.wait_ge(s_rel[k], mine)
                        for j in range(U):
                            last = v.tensor_scalar(oh[k][:, j, :], iota[:, :], rel[:, k, j:j + 1], cols[:, s, 1, j:j + 1], ALU.is_equal, ALU.mult)
                        last.then_inc(s_oh[k], 1)

                    with nc.vector.Fori(0, groups // 4) as i:
                        for n in range(4):
                            g, s, turn = i * 4 + n, n % 2, i * 2 + n // 2
                            first, end = span(v, g)
                            v.wait_ge(s_cols, g + 1)
                            v.wait_ge(s_mm[s], turn + 1)
                            build(first, s, s, turn + 1)
                            with nc.vector.If(end > first + 1):
                                shift = extra(v, g)
                                with nc.vector.Fori(first + 1, end) as a:
                                    v.wait_ge(s_mm[2], shift + a)
                                    build(a, s, 2, shift + a)
                                    v.wait_ge(s_oh[2], shift + a)
                            v.sem_inc(s_mark, 1)
                            v.wait_ge(s_oh[s], turn + 1)
                            v.sem_inc(s_vec, 1)

                @block.tensor
                def _(pe):
                    for a0 in range(0, NB * C, 512):
                        w = min(512, NB * C - a0)
                        last = pe.matmul(sums[:, a0:a0 + w], ident[:, :], acc[:, a0:a0 + w], start=True, stop=True)
                    last.then_inc(s_init, 1)
                    pe.wait_ge(s_init, 1)
                    pe.sem_inc(s_pe, 4)
                    pe.sem_inc(s_mm[0], 1)
                    pe.sem_inc(s_mm[1], 1)
                    pe.sem_inc(s_mm[2], NB + 1)

                    def add(a, n, k):
                        for j in range(U):
                            last = pe.matmul(sums[:, bass.ds(a * C, C)], oh[k][:, j, :], msg[:, n, j, :], start=False, stop=True,
                                             skip_group_check=True)
                        last.then_inc(s_mm[k], 1)

                    with nc.tensor.Fori(0, groups // 4) as i:
                        for n in range(4):
                            g, s, turn = i * 4 + n, n % 2, i * 2 + n // 2
                            first, end = span(pe, g)
                            pe.wait_ge(s_g[n], (i + 1) * (16 * U))
                            pe.sem_inc(s_mark, 1)
                            pe.wait_ge(s_oh[s], turn + 1)
                            add(first, n, s)
                            with nc.tensor.If(end > first + 1):
                                shift = extra(pe, g)
                                with nc.tensor.Fori(first + 1, end) as a:
                                    pe.wait_ge(s_oh[2], shift + a)
                                    add(a, n, 2)
                                pe.wait_ge(s_mm[2], shift + end)
                                pe.sem_inc(s_mark, 1)
                            pe.wait_ge(s_mm[s], turn + 2)
                            pe.sem_inc(s_pe, 1)

        with ExitStack() as c:
            UV = UD - UA
            ohh = c.enter_context(nc.sbuf_tensor("onehot_high", [P, 2, UD, NH], f32))
            ohl = c.enter_context(nc.sbuf_tensor("onehot_low", [P, 2, UD, P2], f32))
            wol = c.enter_context(nc.sbuf_tensor("weighted_low", [P, 2, UD, P2], f32))
            sq = c.enter_context(nc.sbuf_tensor("square", [P, 2, UA, NH], f32))
            xt = c.enter_context(nc.sbuf_tensor("xt", [P, KD, P], f32))
            s_p, s_b, s_wt1, s_sq, s_pa, s_u = (sem(w) for w in (
                "high_onehots", "low_onehots", "weighted", "squares", "high_onehots_act", "degrees_added"))
            s_n, s_t, s_x, s_h, s_a = (sem(w) for w in ("row_normed", "row_transposed", "xt_ready", "h1_psum", "h1_copied"))
            block = c.enter_context(nc.Block())

            def spread(cols, u, n):
                return cols.unsqueeze(2).broadcast_to([P, u, n])

            @block.vector
            def _(v):
                with nc.vector.Fori(0, NB) as i:
                    for s in range(2):
                        g = i * 2 + s
                        v.wait_ge(s_wt1, g + 1)
                        v.tensor_tensor(ohl[:, s, :, :], iota[:, 0:P2].unsqueeze(1).broadcast_to([P, UD, P2]),
                                        spread(dst_low[:, bass.ds(g * UD, UD)], UD, P2), ALU.is_equal).then_inc(s_b, 1)
                        v.wait_ge(s_u, g + 1)
                        v.tensor_tensor(ohh[:, s, 0:UV, :], iota[:, 0:NH].unsqueeze(1).broadcast_to([P, UV, NH]),
                                        spread(dst_high[:, bass.ds(g * UD, UV)], UV, NH), ALU.is_equal).then_inc(s_p, 1)

            @block.gpsimd
            def _(pool):
                with nc.gpsimd.Fori(0, NB) as i:
                    for s in range(2):
                        g = i * 2 + s
                        pool.wait_ge(s_b, g + 1)
                        pool.sem_inc(s_mark, 1)
                        pool.wait_ge(s_u, g + 1)
                        pool.sem_inc(s_mark, 1)
                        pool.tensor_tensor(wol[:, s, :, :], ohl[:, s, :, :], spread(edges[:, 2, bass.ds(g * UD, UD)], UD, P2),
                                           ALU.mult).then_inc(s_wt1, 1)

            @block.scalar
            def _(act):
                def copy_h(t):
                    act.wait_ge(s_h, t + 1)
                    act.activation(acc[:, bass.ds(t * H, H)], bank[1][:, 0:H], ACT.Copy).then_inc(s_a, 1)

                def highs(i, s):
                    g = i * 2 + s
                    act.wait_ge(s_u, g + 1)
                    for j in range(UA):
                        last = act.activation(sq[:, s, j, :], iota[:, 0:NH], ACT.Square, bias=dst_neg[:, bass.ds(g * UD + UV + j, 1)])
                    last.then_inc(s_sq, 1)
                    act.wait_ge(s_sq, g + 1)
                    act.activation(ohh[:, s, UV:UD, :], sq[:, s, :, :], ACT.Relu, bias=ones[:, 0:1], scale=-1.0).then_inc(s_pa, 1)

                act.sem_inc(s_x, 1)
                act.sem_inc(s_a, 1)

                def normalise_row(t):
                    act.activation(xn[:, 0, :], xr[:, bass.ds(t, 1), :].rearrange("p a d -> p (a d)"), ACT.Identity,
                                   bias=nmr[:, bass.ds(t, 1)], scale=rstd[:, bass.ds(t, 1)]).then_inc(s_n, 1)

                def copy_xt(t):
                    act.wait_ge(s_t, t + 1)
                    act.activation(xt[:, :, :], bank[0][:, 0:KD * P].rearrange("p (k c) -> p k c", k=KD), ACT.Copy).then_inc(s_x, 1)

                highs(0, 0)
                with nc.scalar.Fori(0, NB - 1) as i:
                    normalise_row(i)
                    highs(i, 1)
                    copy_xt(i)
                    highs(i + 1, 0)
                    copy_h(i)
                normalise_row(NB - 1)
                highs(NB - 1, 1)
                copy_xt(NB - 1)
                copy_h(NB - 1)

            @block.tensor
            def _(pe):
                pe.matmul(bank[7][0:P2, 0:NH], ident[:, 0:P2], ones[:, 0:NH], start=True, stop=True).then_inc(s_mark, 1)
                pe.sem_inc(s_u, 2)
                pe.sem_inc(s_wt1, 2)

                def degrees(i, s):
                    g = i * 2 + s
                    pe.wait_ge(s_p, g + 1)
                    pe.wait_ge(s_pa, g + 1)
                    pe.wait_ge(s_wt1, g + 3)
                    for j in range(UD):
                        last = pe.matmul(bank[7][0:P2, 0:NH], wol[:, s, j, :], ohh[:, s, j, :], start=False, stop=True, skip_group_check=True)
                    last.then_inc(s_u, 1)

                with nc.tensor.Fori(0, NB) as i:
                    degrees(i, 0)
                    pe.wait_ge(s_n, i + 1)
                    pe.wait_ge(s_x, i + 1)
                    for k in range(KD):
                        last = pe.transpose(bank[0][:, k * P:(k + 1) * P], xn[:, 0, k * P:(k + 1) * P], ident[:, :])
                    last.then_inc(s_t, 1)
                    degrees(i, 1)
                    pe.wait_ge(s_x, i + 2)
                    pe.wait_ge(s_a, i + 1)
                    for k in range(KD):
                        last = pe.matmul(bank[1][:, 0:H], xt[:, k, :], gw1_t[:, k, :], start=(k == 0), stop=(k == KD - 1))
                    last.then_inc(s_h, 1)

        with ExitStack() as c:
            s_v, s_m, s_p, s_d = sem("dis_step"), sem("degree_ready"), sem("degree_root"), sem("table1_stored")
            s_s, s_c = sem("degrees_copied"), sem("degrees_by_block")
            low_high = c.enter_context(nc.sbuf_tensor("degrees", [P2, NH], f32))
            shift = c.enter_context(nc.sbuf_tensor("shift", [P2, P], f32))
            block = c.enter_context(nc.Block())

            @block.tensor
            def _(pe):
                pe.wait_ge(s_s, 1)
                for h, place in enumerate((ident[0:P2, :], shift[:, :])):
                    last = pe.matmul(bank[6][:, 0:NB], place, low_high[:, :].rearrange("r (b h) -> r h b", h=2)[:, h, :], start=(h == 0), stop=(h == 1))
                last.then_inc(s_c, 1)

            @block.vector
            def _(v):
                v.memset(shift[:, 0:P2], 0.0)
                v.tensor_copy(shift[:, P2:P], ident[0:P2, 0:P2])
                v.tensor_copy(low_high[:, :], bank[7][0:P2, 0:NH]).then_inc(s_s, 1)
                v.wait_ge(s_c, 1)
                v.tensor_scalar(tmp[:, :], bank[6][:, 0:NB], 1e-12, None, ALU.max).then_inc(s_m, 1)
                v.tensor_scalar(dis[:, :], bank[6][:, 0:NB], 0.0, None, ALU.is_gt).then_inc(s_v, 1)
                v.wait_ge(s_p, 1)
                v.wait_ge(s_v, 1)
                v.tensor_tensor(dis[:, :], dis[:, :], mv[:, :, 1], ALU.mult).then_inc(s_v, 1)
                v.wait_ge(s_v, 2)
                v.tensor_tensor(acc_of(H), acc_of(H), dis[:, :].unsqueeze(2).broadcast_to([P, NB, H]), ALU.mult).then_inc(s_v, 1)

            @block.gpsimd
            def _(pool):
                pool.wait_ge(s_m, 1)
                pow_neg_half(pool, mv[:, :, 1], tmp[:, :]).then_inc(s_p, 1)

            @block.sync
            def _(sp):
                sp.wait_ge(s_v, 3)
                sp.dma_start(g1_dram.rearrange("(b p) c -> p b c", p=P), acc_of(H)).then_inc(s_d, 16)
                sp.wait_ge(s_d, 16)

        edge_pass("c1", H, g1_dram)

        hT = xT[:, 0, :]

        def finish_conv(name, C, brow):
            with ExitStack() as c:
                s_c, s_t, s_e = sem(f"relu_{name}"), sem(f"hT_psum_{name}"), sem(f"hT_{name}")
                block = c.enter_context(nc.Block())

                @block.vector
                def _(v):
                    a = acc_of(C)
                    v.tensor_tensor(a, sums[:, 0:NB * C].rearrange("p (b c) -> p b c", c=C), dis[:, :].unsqueeze(2).broadcast_to([P, NB, C]), ALU.mult).then_inc(s_c, 1)
                    v.wait_ge(s_c, 1)
                    v.tensor_tensor(a, a, brow[:, :].unsqueeze(1).broadcast_to([P, NB, C]), ALU.add).then_inc(s_c, 1)
                    v.wait_ge(s_c, 2)
                    v.tensor_scalar(a, a, 0.0, None, ALU.max).then_inc(s_c, 1)

                @block.tensor
                def _(pe):
                    pe.wait_ge(s_c, 3)
                    for q, t0 in enumerate(range(0, NB, 4)):
                        if q >= 2:
                            pe.wait_ge(s_e, q - 1)
                        for t in range(t0, min(t0 + 4, NB)):
                            last = pe.transpose(bank[q % 2][0:C, (t - t0) * P:(t - t0 + 1) * P], acc[:, t * C:(t + 1) * C], ident[:, :])
                        last.then_inc(s_t, 1)

                @block.scalar
                def _(act):
                    for q, t0 in enumerate(range(0, NB, 4)):
                        w = min(4, NB - t0) * P
                        act.wait_ge(s_t, q + 1)
                        act.activation(hT[0:C, t0 * P:t0 * P + w], bank[q % 2][0:C, 0:w], ACT.Copy).then_inc(s_e, 1)

        with ExitStack() as c:
            s_c, s_t, s_e, s_m, s_a, s_d = sem("relu_c1"), sem("hT_psum_c1"), sem("hT_c1"), sem("rows_g2"), sem("scaled_g2"), sem("stored_g2")
            block = c.enter_context(nc.Block())
            chunks = [(q, t0, min(4, NB - t0)) for q, t0 in enumerate(range(0, NB, 4))]
            assert NB * H <= 7 * 512 and 2 * 4 * H == 512
            LAG = 4
            spare = [bank[1], bank[2]]

            def turned(q):
                return bank[7] if q % 2 == 0 else bank[0]

            @block.vector
            def _(v):
                def relu(q, t0, n):
                    a = acc[:, t0 * H:(t0 + n) * H].rearrange("p (b c) -> p b c", c=H)
                    d = dis[:, t0:t0 + n].unsqueeze(2).broadcast_to([P, n, H])
                    v.tensor_tensor(a, sums[:, t0 * H:(t0 + n) * H].rearrange("p (b c) -> p b c", c=H), d, ALU.mult).then_inc(s_c, 1)
                    v.wait_ge(s_c, 3 * q + 1)
                    v.tensor_tensor(a, a, b1row[:, :].unsqueeze(1).broadcast_to([P, n, H]), ALU.add).then_inc(s_c, 1)
                    v.wait_ge(s_c, 3 * q + 2)
                    v.tensor_scalar(a, a, 0.0, None, ALU.max).then_inc(s_c, 1)

                def scale(q, t0, n):
                    v.wait_ge(s_m, q + 1)
                    v.tensor_tensor(acc[:, t0 * L:(t0 + n) * L].rearrange("p (b c) -> p b c", c=L),
                                    spare[q % 2][:, 0:n * L].rearrange("p (b c) -> p b c", c=L),
                                    dis[:, t0:t0 + n].unsqueeze(2).broadcast_to([P, n, L]), ALU.mult).then_inc(s_a, 1)
                for chunk in chunks:
                    relu(*chunk)
                    if chunk[0] > LAG:
                        scale(*chunks[chunk[0] - LAG - 1])
                for chunk in chunks[-LAG - 1:]:
                    scale(*chunk)

            @block.tensor
            def _(pe):
                def product(q, t0, n):
                    pe.wait_ge(s_e, q + 1)
                    if q >= 2:
                        pe.wait_ge(s_a, q - 1)
                    for t in range(t0, t0 + n):
                        last = pe.matmul(spare[q % 2][:, (t - t0) * L:(t - t0 + 1) * L], hT[0:H, t * P:(t + 1) * P], gw2_t[:, 0, :], start=True, stop=True)
                    last.then_inc(s_m, 1)
                for q, t0, n in chunks:
                    pe.wait_ge(s_c, 3 * q + 3)
                    if q >= 2:
                        pe.wait_ge(s_e, q - 1)
                    for t in range(t0, t0 + n):
                        last = pe.transpose(turned(q)[0:H, (t - t0) * P:(t - t0 + 1) * P], acc[:, t * H:(t + 1) * H], ident[:, :])
                    last.then_inc(s_t, 1)
                    if q >= LAG:
                        product(*chunks[q - LAG])
                for chunk in chunks[-LAG:]:
                    product(*chunk)

            @block.scalar
            def _(act):
                for q, t0, n in chunks:
                    act.wait_ge(s_t, q + 1)
                    act.activation(hT[0:H, t0 * P:(t0 + n) * P], turned(q)[0:H, 0:n * P], ACT.Copy).then_inc(s_e, 1)

            @block.sync
            def _(sp):
                sp.wait_ge(s_a, len(chunks))
                sp.dma_start(g2_dram.rearrange("(b p) c -> p b c", p=P), acc_of(L)).then_inc(s_d, 16)
                sp.wait_ge(s_d, 16)

        edge_pass("c2", L, g2_dram)
        finish_conv("c2", L, b2row)

        with ExitStack() as c:
            s_d, s_dr, s_y, s_sg, s_x1, s_bn, s_ag, s_var = (sem(w) for w in (
                "d_psum", "d_relu", "xhat_psum", "sigmoid", "x1", "stats2", "aggregated2", "variance2"))
            s_one, s_pw, s_n, s_t, s_e, s_wr = (sem(w) for w in ("ones_row", "rstd2", "normed2", "transposed2", "xT_ready", "wr_in"))
            sg = c.enter_context(nc.sbuf_tensor("sg", [P, 2, D], f32))
            wrt = c.enter_context(nc.sbuf_tensor("wr_sb", [P, KD, NE], f32))
            block = c.enter_context(nc.Block())
            dT = xT[:, 1, :]
            NQ = -(-NP // 512)
            LAG_SIG, LAG_ADD, LAG_STAT, LAG_NORM, LAG_TR, LAG_COPY, LAG_LOG = 1, 2, 3, TS + 4, TS + 5, TS + 6, TS + 7
            steps = range(NB + LAG_LOG)

            def at(n, lag):
                return n - lag if 0 <= n - lag < NB else None

            @block.sync
            def _(sp):
                sp.dma_start(wrt[:, :, :], wr.rearrange("(k p) e -> p k e", p=P)).then_inc(s_wr, 16)
                load_raw(sp, w1s, w2s, s_raw)

            @block.tensor
            def _(pe):
                for q in range(NQ):
                    w = min(512, NP - q * 512)
                    if q >= 2:
                        pe.wait_ge(s_dr, q - 1)
                    pe.matmul(bank[q % 2][0:H, 0:w], wd1t[:, :], hT[0:L, q * 512:q * 512 + w], start=True, stop=True).then_inc(s_d, 1)
                pe.wait_ge(s_one, 1)
                pe.wait_ge(s_dr, NQ)
                pe.wait_ge(s_wr, 16)

                for n in steps:
                    t = at(n, 0)
                    if t is not None:
                        if t >= 2:
                            pe.wait_ge(s_sg, t - 1)
                        pe.matmul(bank[2 + t % 2][:, 0:D], dT[0:H + 1, t * P:(t + 1) * P], wd2t[:, :], start=True, stop=True).then_inc(s_y, 1)
                    t = at(n, LAG_TR)
                    if t is not None:
                        pe.wait_ge(s_n, t + 1)
                        if t >= 2:
                            pe.wait_ge(s_e, t - 1)
                        for k in range(KD):
                            last = pe.transpose(bank[4 + t % 2][:, k * P:(k + 1) * P], xn[:, t % 2, k * P:(k + 1) * P], ident[:, :])
                        last.then_inc(s_t, 1)
                    t = at(n, LAG_LOG)
                    if t is not None:
                        pe.wait_ge(s_e, t + 1)
                        for k in range(KD):
                            pe.matmul(bank[6][:, t * NE:(t + 1) * NE], xT[:, k, t * P:(t + 1) * P], wrt[:, k, :],
                                      start=(k == 0), stop=(k == KD - 1))

            @block.scalar
            def _(act):
                for q in range(NQ):
                    w = min(512, NP - q * 512)
                    act.wait_ge(s_d, q + 1)
                    act.activation(dT[0:H, q * 512:q * 512 + w], bank[q % 2][0:H, 0:w], ACT.Relu, bias=bd1c[:, :]).then_inc(s_dr, 1)
                for n in steps:
                    t = at(n, LAG_SIG)
                    if t is not None:
                        act.wait_ge(s_y, t + 1)
                        if t >= 2:
                            act.wait_ge(s_x1, t - 1)
                        act.activation(sg[:, t % 2, :], bank[2 + t % 2][:, 0:D], ACT.Sigmoid).then_inc(s_sg, 1)
                    t = at(n, LAG_COPY)
                    if t is not None:
                        act.wait_ge(s_t, t + 1)
                        act.activation(xT[:, :, t * P:(t + 1) * P], bank[4 + t % 2][:, 0:KD * P].rearrange("p (k c) -> p k c", k=KD),
                                       ACT.Copy).then_inc(s_e, 1)

            @block.vector
            def _(v):
                v.memset(dT[H:H + 1, :], 1.0).then_inc(s_one, 1)
                for n in steps:
                    t = at(n, LAG_NORM)
                    if t is not None:
                        if t % TS == 0:
                            v.wait_ge(s_pw, t // TS + 1)
                        if t >= 2:
                            v.wait_ge(s_t, t - 1)
                        v.tensor_scalar(xn[:, t % 2, :], xr[:, t, :], mv[:, t, 0:1], rstd[:, t:t + 1], ALU.subtract, ALU.mult).then_inc(s_n, 1)
                    t = at(n, LAG_ADD)
                    if t is not None:
                        v.wait_ge(s_sg, t + 1)
                        v.tensor_tensor(xr[:, t, :], xr[:, t, :], sg[:, t % 2, :], ALU.add).then_inc(s_x1, 1)
                    t = at(n, LAG_STAT)
                    if t is not None:
                        v.wait_ge(s_x1, t + 1)
                        v.bn_stats(stat[:, t, :], xr[:, t, :]).then_inc(s_bn, 1)
                        if t % TS == TS - 1:
                            v.wait_ge(s_bn, t + 1)
                            for j in range(t - TS + 1, t + 1):
                                last = v.bn_aggr(mv[:, j, :], stat[:, j, :])
                            last.then_inc(s_ag, 1)
                            v.wait_ge(s_ag, t // TS + 1)
                            v.tensor_scalar(tmp[:, t - TS + 1:t + 1], mv[:, t - TS + 1:t + 1, 1], EPS, None, ALU.add).then_inc(s_var, 1)

            @block.gpsimd
            def _(pool):
                for g in range(NT):
                    pool.wait_ge(s_var, g + 1)
                    r = slice(g * TS, (g + 1) * TS)
                    pool.tensor_tensor(rstd[:, r], tmp[:, r], half[:, r], ALU.pow).then_inc(s_pw, 1)

        graph.close()
        UPPER, LOWER = 0, 1
        shared = ExitStack()
        w1 = shared.enter_context(nc.sbuf_tensor("w1s_parts", [P, 2, KD, F], f32r))
        w2 = shared.enter_context(nc.sbuf_tensor("w2s_parts", [P, 2, KF, D], f32r))

        with ExitStack() as c:
            def sbr(name, shape, dt=f32):
                return c.enter_context(nc.sbuf_tensor(name, shape, dt))
            lg = sbr("lg", [P, NB, NE])
            m8 = sbr("m8", [P, NB, NE])
            i8 = sbr("i8", [P, NB, NE], u32)
            i8f = sbr("i8f", [P, NB, 2])
            dl = sbr("dl", [P, NB, 2])
            eq = sbr("eq", [P, 2, NB, NE])
            both = sbr("both", [P, NB, NE])
            slot = sbr("slot", [P, NB, NE])
            upto = sbr("upto", [P, NE, NB])
            prod = sbr("prod", [P, NB, NE])
            zer = sbr("zer_row", [P, NB])
            nu = sbr("nu", [P, NE])
            nui = sbr("nui", [P, NE], i32)
            uend = sbr("uend", [P, NE])
            ei = sbr("ei", [P, NE], i32)
            ef = sbr("ef", [P, NE])
            b1r = sbr("b1r", [(NE + 1) * KF, P])
            s_bt, s_both, s_cnt = sem("biases_transposed"), sem("choices"), sem("counts")
            s_w, s_i, s_ch, s_dl, s_wt = sem("ffn_biases_in"), sem("expert_ids"), sem("routerchain"), sem("gap"), sem("topw_set")
            block = c.enter_context(nc.Block())

            @block.sync
            def _(sp):
                sp.dma_start(b1r[0:NE * KF, :], b1p.rearrange("e (k p) -> (e k) p", p=P)).then_inc(s_w, 16)
                sp.dma_start(b1r[NE * KF:(NE + 1) * KF, :], b1s.rearrange("(k p) -> k p", p=P)).then_inc(s_w, 16)

            @block.gpsimd
            def _(pool):
                pool.memset(zer[:, :], 0.0)
                pool.iota(ei[:, :], pattern=[[1, NE]], base=0, channel_multiplier=0).then_inc(s_i, 1)

            @block.tensor
            def _(pe):
                pe.wait_ge(s_w, 32)
                pe.transpose(bank[1][:, 0:(NE + 1) * KF], b1r[:, :], ident[0:(NE + 1) * KF, 0:(NE + 1) * KF]).then_inc(s_bt, 1)
                pe.wait_ge(s_both, 1)
                pe.matmul(bank[2][:, 0:NB * NE], tri[:, :], both[:, :, :].rearrange("p b e -> p (b e)"), start=True, stop=True)
                pe.matmul(bank[3][:, 0:NB * NE], ones[:, :], both[:, :, :].rearrange("p b e -> p (b e)"), start=True, stop=True).then_inc(s_cnt, 1)

            @block.scalar
            def _(act):
                act.wait_ge(s_raw, 32)
                act.activation(w1[:, UPPER, :, :], raw1[:, :, :], ACT.Copy).then_inc(s_split_u, 1)
                act.activation(w2[:, UPPER, :, :], raw2[:, :, :], ACT.Copy).then_inc(s_split_u, 1)
                act.wait_ge(s_dl, 1)
                act.activation(topw[:, :, :], dl[:, :, :], ACT.Sigmoid).then_inc(s_wt, 1)

            @block.vector
            def _(v):
                n = [0]

                def link(ins):
                    n[0] += 1
                    ins.then_inc(s_ch, 1)
                    v.wait_ge(s_ch, n[0])
                link(v.tensor_copy(lg[:, :, :], bank[6][:, 0:NB * NE].rearrange("p (t e) -> p t e", e=NE)))
                for t in range(NB):
                    last = v.max(m8[:, t, :], lg[:, t, :])
                link(last)
                for t in range(NB):
                    last = v.max_index(i8[:, t, :], m8[:, t, :], lg[:, t, :])
                link(last)
                link(v.tensor_copy(i8f[:, :, :], i8[:, :, 0:2]))
                link(v.tensor_tensor(dl[:, :, 0], m8[:, :, 0], m8[:, :, 1], ALU.subtract))
                v.tensor_tensor(dl[:, :, 1], m8[:, :, 1], m8[:, :, 0], ALU.subtract).then_inc(s_dl, 1)
                v.wait_ge(s_i, 1)
                link(v.tensor_copy(ef[:, :], ei[:, :]))
                for k in range(2):
                    last = v.tensor_tensor(eq[:, k, :, :], ef[:, :].unsqueeze(1).broadcast_to([P, NB, NE]), i8f[:, :, k:k + 1].broadcast_to([P, NB, NE]), ALU.is_equal)
                link(last)
                link(v.tensor_tensor(both[:, :, :], eq[:, 0, :, :], eq[:, 1, :, :], ALU.add))
                v.tensor_scalar(both[:, NB - 1, :], both[:, NB - 1, :], valid[:, :], None, ALU.mult).then_inc(s_both, 1)
                v.wait_ge(s_split_u, 2)
                v.tensor_tensor(w1[:, LOWER, :, :], raw1[:, :, :], w1[:, UPPER, :, :].bitcast(f32), ALU.subtract)
                v.tensor_tensor(w2[:, LOWER, :, :], raw2[:, :, :], w2[:, UPPER, :, :].bitcast(f32), ALU.subtract).then_inc(s_split, 1)
                v.wait_ge(s_bt, 1)
                v.tensor_copy(b1t[:, :], bank[1][:, 0:(NE + 1) * KF])
                v.wait_ge(s_cnt, 1)
                count = bank[3][:, 0:NB * NE].rearrange("p (b e) -> p b e", e=NE)
                for e in range(NE):
                    last = v.tensor_tensor_scan(upto[:, e, :], count[:, :, e], zer[:, :], 0.0, ALU.add, ALU.add)
                link(last)
                link(v.tensor_scalar(nu[:, :], upto[:, :, NB - 1], 1.0, float(UT - 1), ALU.max, ALU.add))
                link(v.tensor_copy(nui[:, :], nu[:, :]))
                link(v.tensor_scalar(nui[:, :], nui[:, :], UT.bit_length() - 1, None, ALU.arith_shift_right))
                link(v.tensor_copy(nu[:, :], nui[:, :]))
                link(v.tensor_tensor_scan(uend[:, :], nu[:, :], zer[:, 0:NE], 0.0, ALU.add, ALU.add))
                link(v.tensor_copy(ends[:, :], uend[0:1, :]))
                link(v.tensor_tensor(nu[:, :], uend[:, :], nu[:, :], ALU.subtract))
                link(v.tensor_scalar(nu[:, :], nu[:, :], float(UT), None, ALU.mult))
                link(v.tensor_tensor(slot[:, :, :], upto[:, :, :].rearrange("p e b -> p b e"), count, ALU.subtract))
                link(v.tensor_tensor(slot[:, :, :], slot[:, :, :], bank[2][:, 0:NB * NE].rearrange("p (b e) -> p b e", e=NE), ALU.add))
                link(v.tensor_tensor(slot[:, :, :], slot[:, :, :], nu[:, :].unsqueeze(1).broadcast_to([P, NB, NE]), ALU.add))
                for k in range(2):
                    link(v.tensor_tensor(prod[:, :, :], slot[:, :, :], eq[:, k, :, :], ALU.mult))
                    link(v.tensor_reduce(slots[:, :, k], prod[:, :, :], AX.X, ALU.add))

        KQ = KF // 4

        class Unit:
            def __init__(self, c, name):
                def t(n, shape, dt=f32r):
                    return c.enter_context(nc.sbuf_tensor(f"{n}_{name}", shape, dt))
                self.x = t("x_parts", [P, 2, KD, UT])
                self.g = t("gelu_out", [P, KF, UT], f32)
                self.h = t("h_parts", [P, 2, KF, UT])
                self.s_x, self.s_h, self.s_g, self.s_hu, self.s_hr, self.s_y, self.s_yd = (sem(f"{w}_{name}") for w in (
                    "x_split", "h_psum", "gelu", "h_upper", "h_rest", "y_psum", "y_taken"))

            def up(self, pe, u, w1, W=UT):
                pe.wait_ge(self.s_x, u + 1)
                for q in range(4):
                    for f in range(q * KQ, (q + 1) * KQ):
                        n = 0
                        for k in range(KD):
                            for wp, xp in ((UPPER, UPPER), (LOWER, UPPER), (UPPER, LOWER)):
                                n += 1
                                last = pe.matmul(bank[q][:, (f % KQ) * UT:(f % KQ) * UT + W], w1[:, wp, k, f * P:(f + 1) * P],
                                                 self.x[:, xp, k, 0:W], start=(n == 1), stop=(n == 3 * KD))
                    last.then_inc(self.s_h, 1)

            def down(self, pe, u, w2, W=UT):
                pe.wait_ge(self.s_yd, u + 1)
                for q in range(4):
                    pe.wait_ge(self.s_hr, u * 4 + q + 1)
                    for h in range(W // P):
                        for f in range(q * KQ, (q + 1) * KQ):
                            for n, (hp, wp) in enumerate(((UPPER, UPPER), (LOWER, UPPER), (UPPER, LOWER))):
                                last = pe.matmul(bank[5 + h][:, 0:D], self.h[:, hp, f, h * P:(h + 1) * P], w2[:, wp, f, :],
                                                 start=(f == 0 and n == 0), stop=(f == KF - 1 and n == 2))
                last.then_inc(self.s_y, 1)

            def gelu(self, act, u, e, W=UT):
                for q in range(4):
                    act.wait_ge(self.s_h, u * 4 + q + 1)
                    for f in range(q * KQ, (q + 1) * KQ):
                        last = act.activation(self.g[:, f, 0:W], bank[q][:, (f % KQ) * UT:(f % KQ) * UT + W], ACT.Gelu,
                                              bias=b1t[:, e * KF + f:e * KF + f + 1])
                    last.then_inc(self.s_g, 1)
                    act.wait_ge(self.s_g, u * 4 + q + 1)
                    act.activation(self.h[:, UPPER, q * KQ:(q + 1) * KQ, 0:W], self.g[:, q * KQ:(q + 1) * KQ, 0:W], ACT.Copy).then_inc(self.s_hu, 1)

            def rests(self, v, u, W=UT):
                for q in range(4):
                    v.wait_ge(self.s_hu, u * 4 + q + 1)
                    f = slice(q * KQ, (q + 1) * KQ)
                    v.tensor_tensor(self.h[:, LOWER, f, 0:W], self.g[:, f, 0:W], self.h[:, UPPER, f, 0:W].bitcast(f32), ALU.subtract).then_inc(self.s_hr, 1)

        with normal, shared, ExitStack() as c:
            TG1 = 2
            STEPS1 = (NB - 1) // TG1
            assert NB - 1 == TG1 * STEPS1
            b2s_t = c.enter_context(nc.sbuf_tensor("b2s_sb", [P, D], f32))
            xn4 = c.enter_context(nc.sbuf_tensor("xn4", [P, TG1, D], f32))
            idx = c.enter_context(nc.sbuf_tensor("slot_of", [P, TG1, 2], u32))
            zeros = c.enter_context(nc.sbuf_tensor("zeros", [P, 2, D], f32))
            s_b2, s_zs, s_z, s_zy, s_n, s_xu, s_b = sem("shared_bias_in"), sem("zeros_set"), sem("tails_zeroed"), sem("unused_zeroed"), sem("normed"), sem("rows_upper"), sem("bias_added")
            s_sc = [sem(f"scattered{j}") for j in range(TG1)]
            sh = Unit(c, "shared")
            block = c.enter_context(nc.Block())

            @block.sync
            def _(sp):
                load_raw(sp, w1p[0], w2p[0], s_raw)
                sp.dma_start(b2s_t[:, :], b2s.rearrange("(o d) -> o d", o=1).broadcast_to([P, D])).then_inc(s_b2, 16)
                sp.wait_ge(s_zs, 1)
                for e in range(NE):
                    end = sp.value_load(ends[0:1, e:e + 1], min_val=1, max_val=UMAX)
                    sp.dma_start(x_dram[bass.ds((end - 1) * UT, UT), :].rearrange("(h p) d -> p h d", p=P), zeros[:, :, :]).then_inc(s_z, 16)
                sp.dma_start(x_dram[bass.ds(end * UT, UT), :].rearrange("(h p) d -> p h d", p=P), zeros[:, :, :]).then_inc(s_z, 16)
                with nc.sync.Fori(end, UMAX + 1) as u:
                    sp.dma_start(y_dram[bass.ds(u * UT, UT), :].rearrange("(h p) d -> p h d", p=P), zeros[:, :, :]).then_inc(s_zy, 16)
                sp.wait_ge(s_z, 16 * (NE + 1))
                with nc.sync.Fori(0, end) as u:
                    sp.sem_inc(s_zy, 16)
                sp.wait_ge(s_zy, (UMAX + 1) * 16)

            @block.tensor
            def _(pe):
                pe.sem_inc(sh.s_yd, 1)
                with nc.tensor.Fori(0, STEPS1) as i:
                    sh.up(pe, i, w1)
                    sh.down(pe, i, w2)
                sh.up(pe, STEPS1, w1, P)
                sh.down(pe, STEPS1, w2, P)

            @block.scalar
            def _(act):
                with nc.scalar.Fori(0, STEPS1) as i:
                    sh.gelu(act, i, NE)
                sh.gelu(act, STEPS1, NE, P)

            @block.vector
            def _(v):
                v.memset(zeros[:, :, :], 0.0).then_inc(s_zs, 1)

                def split_x(u, t, W=UT):
                    if not isinstance(u, int) or u > 0:
                        v.wait_ge(sh.s_h, u * 4)
                    rows = xT[:, :, bass.ds(t * P, W)]
                    v.tensor_copy(sh.x[:, UPPER, :, 0:W], rows).then_inc(s_xu, 1)
                    v.wait_ge(s_xu, u + 1)
                    v.tensor_tensor(sh.x[:, LOWER, :, 0:W], rows, sh.x[:, UPPER, :, 0:W].bitcast(f32), ALU.subtract).then_inc(sh.s_x, 1)

                def prepare(i, j, t):
                    if not isinstance(i, int) or i > 0:
                        v.wait_ge(s_sc[j], i * 32)
                    v.tensor_copy(idx[:, j, :], slots[:, bass.ds(t, 1), :].rearrange("p a k -> p (a k)"))
                    v.tensor_scalar(xn4[:, j, :], xr[:, bass.ds(t, 1), :].rearrange("p a d -> p (a d)"),
                                    mv[:, bass.ds(t, 1), 0:1].rearrange("p a b -> p (a b)"),
                                    rstd[:, bass.ds(t, 1)], ALU.subtract, ALU.mult).then_inc(s_n, 1)

                def add(u, t, W=UT):
                    for h in range(W // P):
                        o = xr[:, bass.ds(t + h, 1), :].rearrange("p a d -> p (a d)")
                        last = v.tensor_tensor(o, o, b2s_t[:, :], ALU.add)
                    last.then_inc(s_b, 1)
                    v.wait_ge(s_b, u + 1)
                    v.wait_ge(sh.s_y, u + 1)
                    for h in range(W // P):
                        o = xr[:, bass.ds(t + h, 1), :].rearrange("p a d -> p (a d)")
                        last = v.tensor_tensor(o, bank[5 + h][:, 0:D], o, ALU.add)
                    last.then_inc(sh.s_yd, 1)
                for j in range(TG1):
                    prepare(0, j, j)
                split_x(0, 0)
                v.wait_ge(s_b2, 16)
                with nc.vector.Fori(0, STEPS1 - 1) as i:
                    sh.rests(v, i)
                    split_x(i + 1, i * 2 + 2)
                    add(i, i * 2)
                    for j in range(TG1):
                        prepare(i + 1, j, i * TG1 + TG1 + j)
                prepare(STEPS1, 0, NB - 1)
                sh.rests(v, STEPS1 - 1)
                split_x(STEPS1, NB - 1, P)
                add(STEPS1 - 1, NB - 3)
                sh.rests(v, STEPS1, P)
                add(STEPS1, NB - 1, P)

            @block.gpsimd
            def _(pool):
                pool.wait_ge(s_z, 16 * (NE + 1))

                def scatter(n, j, rows):
                    pool.wait_ge(s_n, n + 1)
                    pool.sem_inc(s_mark, 1)
                    for k in range(2):
                        pool.indirect_dma_start(out=x_dram, out_offset=bass.IndirectOffsetOnAxis(ap=idx[0:rows, j, k:k + 1], axis=0),
                                                in_=xn4[0:rows, j, :], in_offset=None).then_inc(s_sc[j], 16)
                with nc.gpsimd.Fori(0, STEPS1) as i:
                    for j in range(TG1):
                        scatter(i * TG1 + j, j, P)
                scatter(NB - 1, 0, LASTB)
                for j in range(TG1):
                    pool.wait_ge(s_sc[j], 32 * (STEPS1 + (j == 0)))

        with ExitStack() as c:
            w1 = c.enter_context(nc.sbuf_tensor("w1_parts", [P, 2, 2, KD, F], f32r))
            w2 = c.enter_context(nc.sbuf_tensor("w2_parts", [P, 2, 2, KF, D], f32r))
            b2t = c.enter_context(nc.sbuf_tensor("b2_sb", [P, 2, D], f32))
            xin = c.enter_context(nc.sbuf_tensor("xin", [P, 2, D], f32))
            ysb = c.enter_context(nc.sbuf_tensor("ysb", [P, 2, D], f32))
            s_w = [sem(f"expert_ready{k}") for k in range(2)]
            s_b2 = [sem(f"expert_bias{k}") for k in range(2)]
            s_xin, s_t, s_xu, s_st, s_praw, s_pu = (sem(w) for w in (
                "unit_in", "unit_transposed", "unit_upper", "unit_stored", "raw_in_pool", "weights_upper_pool"))
            un = Unit(c, "routed")
            block = c.enter_context(nc.Block())

            def expert_end(eng, e):
                return eng.value_load(ends[0:1, e:e + 1], min_val=1, max_val=UMAX)

            def unit(table, u):
                return table[bass.ds(u * UT, UT), :].rearrange("(h p) d -> p h d", p=P)

            @block.gpsimd
            def _(pool):
                def bias(e):
                    pool.dma_start(b2t[:, e % 2, :], b2p[e].rearrange("(o d) -> o d", o=1).broadcast_to([P, D])).then_inc(s_b2[e % 2], 16)
                bias(0)
                pool.wait_ge(s_w[0], 2)
                for e in range(1, NE):
                    load_raw(pool, w1p[e], w2p[e], s_praw)
                    if e >= 2:
                        pool.wait_ge(un.s_yd, expert_end(pool, e - 2) + 1)
                        pool.sem_inc(s_mark, 1)
                    bias(e)
                    pool.wait_ge(s_praw, 32 * e)
                    for k, (w, raw) in enumerate(((w1, raw1), (w2, raw2))):
                        pool.tensor_copy(w[:, e % 2, UPPER, :, :], raw[:, :, :]).then_inc(s_pu, 1)
                        pool.wait_ge(s_pu, 4 * (e - 1) + 2 * k + 1)
                        pool.tensor_tensor(w[:, e % 2, LOWER, :, :], raw[:, :, :], w[:, e % 2, UPPER, :, :].bitcast(f32), ALU.subtract).then_inc(s_pu, 1)
                    pool.wait_ge(s_pu, 4 * e)
                    pool.sem_inc(s_w[e % 2], 2)

            @block.sync
            def _(sp):
                sp.dma_start(xin[:, :, :], unit(x_dram, 0)).then_inc(s_xin, 16)
                total = expert_end(sp, NE - 1)
                with nc.sync.Fori(0, total) as u:
                    sp.wait_ge(s_t, u + 1)
                    sp.dma_start(xin[:, :, :], unit(x_dram, u + 1)).then_inc(s_xin, 16)
                    sp.wait_ge(un.s_yd, u + 2)
                    sp.dma_start(unit(y_dram, u), ysb[:, :, :]).then_inc(s_st, 16)
                sp.wait_ge(s_st, total * 16 + 16)
                sp.sem_inc(s_mark, 1)

            @block.tensor
            def _(pe):
                pe.sem_inc(un.s_yd, 1)

                def transposes(n):
                    pe.wait_ge(s_xin, n * 16 + 16)
                    for h in range(2):
                        for k in range(KD):
                            last = pe.transpose(bank[4][:, k * UT + h * P:k * UT + (h + 1) * P], xin[:, h, k * P:(k + 1) * P], ident[:, :])
                    last.then_inc(s_t, 1)
                transposes(0)
                first = 0
                for e in range(NE):
                    s = e % 2
                    end = expert_end(pe, e)
                    pe.wait_ge(s_w[s], 2 * (e // 2 + 1))
                    with nc.tensor.Fori(first, end) as u:
                        un.up(pe, u, w1[:, s, :, :, :])
                        transposes(u + 1)
                        un.down(pe, u, w2[:, s, :, :, :])
                    first = end

            @block.scalar
            def _(act):
                act.wait_ge(s_raw, 64)
                act.activation(w1[:, 0, UPPER, :, :], raw1[:, :, :], ACT.Copy).then_inc(s_split_u, 1)
                act.activation(w2[:, 0, UPPER, :, :], raw2[:, :, :], ACT.Copy).then_inc(s_split_u, 1)
                first = 0
                for e in range(NE):
                    end = expert_end(act, e)
                    with nc.scalar.Fori(first, end) as u:
                        un.gelu(act, u, e)
                    first = end

            @block.vector
            def _(v):
                v.sem_inc(s_st, 16)

                def take(n):
                    v.wait_ge(s_t, n + 1)
                    rows = bank[4][:, 0:KD * UT].rearrange("p (k c) -> p k c", k=KD)
                    v.tensor_copy(un.x[:, UPPER, :, :], rows).then_inc(s_xu, 1)
                    v.wait_ge(s_xu, n + 1)
                    v.tensor_tensor(un.x[:, LOWER, :, :], rows, un.x[:, UPPER, :, :].bitcast(f32), ALU.subtract).then_inc(un.s_x, 1)
                take(0)
                v.wait_ge(s_split_u, 4)
                v.tensor_tensor(w1[:, 0, LOWER, :, :], raw1[:, :, :], w1[:, 0, UPPER, :, :].bitcast(f32), ALU.subtract).then_inc(s_w[0], 1)
                v.tensor_tensor(w2[:, 0, LOWER, :, :], raw2[:, :, :], w2[:, 0, UPPER, :, :].bitcast(f32), ALU.subtract).then_inc(s_w[0], 1)
                first = 0
                for e in range(NE):
                    end = expert_end(v, e)
                    v.wait_ge(s_b2[e % 2], 16 * (e // 2 + 1))
                    with nc.vector.Fori(first, end) as u:
                        un.rests(v, u)
                        take(u + 1)
                        v.wait_ge(s_st, u * 16 + 16)
                        v.wait_ge(un.s_y, u + 1)
                        for h in range(2):
                            last = v.tensor_tensor(ysb[:, h, :], bank[5 + h][:, 0:D], b2t[:, e % 2, :], ALU.add)
                        last.then_inc(un.s_yd, 1)
                    first = end

        with ExitStack() as c:
            TG = 8
            STEPS = (NB - 1) // TG
            assert NB - 1 == TG * STEPS
            got = c.enter_context(nc.sbuf_tensor("got", [P, TG, 2, D], f32))
            idx = c.enter_context(nc.sbuf_tensor("result_of", [P, TG, 2], u32))
            s_ix, s_cm, s_sv = sem("result_slots"), sem("combined"), sem("out_stored")
            s_g = [sem(f"results_in{j}") for j in range(TG)]
            block = c.enter_context(nc.Block())

            @block.gpsimd
            def _(pool):
                def gather(n, j, rows):
                    pool.wait_ge(s_ix, n + 1)
                    pool.sem_inc(s_mark, 1)
                    for k in range(2):
                        pool.indirect_dma_start(out=got[0:rows, j, k, :], out_offset=None, in_=y_dram,
                                                in_offset=bass.IndirectOffsetOnAxis(ap=idx[0:rows, j, k:k + 1], axis=0)).then_inc(s_g[j], 16)
                with nc.gpsimd.Fori(0, STEPS) as i:
                    for j in range(TG):
                        gather(i * TG + j, j, P)
                gather(NB - 1, 0, LASTB)

            @block.vector
            def _(v):
                def request(t, j):
                    v.tensor_copy(idx[:, j, :], slots[:, bass.ds(t, 1), :].rearrange("p a k -> p (a k)")).then_inc(s_ix, 1)

                def combine(i, j, t, rows=P):
                    v.wait_ge(s_g[j], i * 32 + 32)
                    o = xr[0:rows, bass.ds(t, 1), :].rearrange("p a d -> p (a d)")
                    for k in range(2):
                        w = topw[0:rows, bass.ds(t, 1), k:k + 1].rearrange("p a b -> p (a b)")
                        v.scalar_tensor_tensor(out=o, in0=got[0:rows, j, k, :], scalar=w, in1=o, op0=ALU.mult, op1=ALU.add).then_inc(s_cm, 1)
                        v.wait_ge(s_cm, t * 2 + k + 1)
                for j in range(TG):
                    request(j, j)
                with nc.vector.Fori(0, STEPS - 1) as i:
                    for j in range(TG):
                        combine(i, j, i * TG + j)
                        request(i * TG + TG + j, j)
                for j in range(TG):
                    combine(STEPS - 1, j, (STEPS - 1) * TG + j)
                    if j == 0:
                        request(NB - 1, 0)
                combine(STEPS, 0, NB - 1, LASTB)

            @block.sync
            def _(sp):
                with nc.sync.Fori(0, STEPS) as i:
                    sp.wait_ge(s_cm, i * (2 * TG) + 2 * TG)
                    sp.dma_start(out[bass.ds(i * (TG * P), TG * P), :].rearrange("(b p) d -> p b d", p=P),
                                 xr[:, bass.ds(i * TG, TG), :]).then_inc(s_sv, 16)
                sp.wait_ge(s_cm, 2 * NB)
                sp.dma_start(out[(NB - 1) * P:N, :], xr[0:LASTB, NB - 1, :]).then_inc(s_sv, 16)
                sp.wait_ge(s_sv, 16 * (STEPS + 1))


_INS = ['x', 'src', 'dst', 'edge_weight', 'L0_gnn_W1', 'L0_gnn_b1', 'L0_gnn_W2', 'L0_gnn_b2', 'L0_gnn_Wd1', 'L0_gnn_bd1',
        'L0_gnn_Wd2', 'L0_gnn_bd2', 'L0_ffn_Wr', 'L0_ffn_W1s', 'L0_ffn_b1s', 'L0_ffn_W2s', 'L0_ffn_b2s', 'L0_ffn_W1p',
        'L0_ffn_b1p', 'L0_ffn_W2p', 'L0_ffn_b2p']


def kernel(**inputs):
    import numpy as _np
    import concourse.bacc as _bacc
    from concourse import mybir as _mybir
    from concourse.bass_utils import run_bass_kernel_spmd as _run

    nc = _bacc.Bacc("TRN2", target_bir_lowering=False, num_devices=1)
    arrays, args = {}, []
    for name in _INS:
        a = _np.ascontiguousarray(inputs[name])
        arrays[f"in_{name}_dram"] = a
        args.append(nc.dram_tensor(f"in_{name}_dram", a.shape, _mybir.dt.from_np(a.dtype), kind="ExternalInput").ap())
    shape = inputs['x'].shape
    args.append(nc.dram_tensor("out_0_dram", tuple(shape), _mybir.dt.float32, kind="ExternalOutput").ap())
    gnn_moe_kernel(nc, *args)
    r = _run(nc, [arrays], core_ids=[0])
    return r.results[0]["out_0_dram"]
```
